# Optimizing a Trainium2 kernel written in Bass

```python
import numpy as np
import jax
import jax.numpy as jnp

def _softmax(x, axis=-1):
    return jax.nn.softmax(x, axis=axis)

def _gelu(x):
    return jax.nn.gelu(x, approximate=True)

def _silu(x):
    return jax.nn.silu(x)

def _sigmoid(x):
    return jax.nn.sigmoid(x)

def _layernorm(x, axis=-1, eps=1e-05):
    m = jnp.mean(x, axis=axis, keepdims=True)
    v = jnp.var(x, axis=axis, keepdims=True)
    return (x - m) / jnp.sqrt(v + eps)

def _scatter_add(tgt, idx, src, axis=0):
    return tgt.at[idx].add(src)

def _segment_sum(src, seg, n):
    return jax.ops.segment_sum(src, seg, n)
kernel_name = 'mk_audio_tower_d1_tok_audfeat512_r4_345cf1'

def setup_inputs(seed: int=0):
    np.random.seed(seed)
    _w = jnp.asarray

    def _rec_inputs():
        import jax
        import jax.numpy as jnp
        _rk = jax.random.key(seed)
        x = -6.41493e-05 + 1.00002 * jax.random.normal(jax.random.fold_in(_rk, 1), (8, 750, 80), jnp.float32)
        return x
    x = _rec_inputs()

    def _L0_tok_setup():
        import jax, jax.numpy as jnp
        import numpy as np
        CTX = np.array([-2, -1, 0, 1, 2])
        STRIDE = 1
        EPS = 1e-05
        key = jax.random.key(seed)
        k1, k2, k3 = jax.random.split(key, 3)
        B, L, D = (64, 500, 80)
        O, K = (128, D * len(CTX))
        x = jax.random.normal(k1, (B, L, D), dtype=jnp.float32)
        W = jax.random.normal(k2, (O, K), dtype=jnp.float32) * (1.0 / np.sqrt(K))
        b = jax.random.normal(k3, (O,), dtype=jnp.float32) * 0.01
        gamma = jnp.ones((O,), dtype=jnp.float32)
        beta = jnp.zeros((O,), dtype=jnp.float32)
        return {'x': x, 'W': W, 'b': b, 'gamma': gamma, 'beta': beta}
    _L0_tok_all = _L0_tok_setup()
    _L0_tok_in = {k: v for k, v in _L0_tok_all.items() if k in ('W', 'b', 'gamma', 'beta')}
    del _L0_tok_all

    def _L0_attn_setup():
        import jax, jax.numpy as jnp
        import numpy as np
        key = jax.random.key(seed)
        x = jax.random.normal(key, (4, 1024, 128), dtype=jnp.float32)
        return {'x': x}
    _L0_attn_all = _L0_attn_setup()
    _L0_attn_in = {k: v for k, v in _L0_attn_all.items() if k in ()}
    del _L0_attn_all

    def _L0_ffn_setup():
        import jax, jax.numpy as jnp
        import numpy as np

        def _haar_dwt2(x):
            a = x[:, ::2, ::2]
            b = x[:, ::2, 1::2]
            c = x[:, 1::2, ::2]
            d = x[:, 1::2, 1::2]
            ll = (a + b + c + d) * 0.5
            lh = (a + b - c - d) * 0.5
            hl = (a - b + c - d) * 0.5
            hh = (a - b - c + d) * 0.5
            return (ll, lh, hl, hh)

        def _haar_idwt2(ll, lh, hl, hh):
            a = (ll + lh + hl + hh) * 0.5
            b = (ll + lh - hl - hh) * 0.5
            c = (ll - lh + hl - hh) * 0.5
            d = (ll - lh - hl + hh) * 0.5
            B, H2, W2 = ll.shape
            out = jnp.zeros((B, 2 * H2, 2 * W2), ll.dtype)
            out = out.at[:, ::2, ::2].set(a)
            out = out.at[:, ::2, 1::2].set(b)
            out = out.at[:, 1::2, ::2].set(c)
            out = out.at[:, 1::2, 1::2].set(d)
            return out

        def _interp_linear_last(x, m):
            n = x.shape[-1]
            pos = jnp.linspace(0.0, 1.0, m, dtype=x.dtype) * (n - 1)
            i0 = jnp.clip(jnp.floor(pos).astype(jnp.int32), 0, n - 2)
            w = pos - i0.astype(x.dtype)
            return x[..., i0] * (1.0 - w) + x[..., i0 + 1] * w
        key = jax.random.key(seed)
        k0, k1, k2 = jax.random.split(key, 3)
        b, f, c, hidden = (128, 64, 128, 512)
        x = jax.random.normal(k0, (b, f, c), dtype=jnp.float32)
        fc1_w = jax.random.normal(k1, (hidden, c), dtype=jnp.float32) * 0.02
        fc1_b = jnp.zeros((hidden,), dtype=jnp.float32)
        fc2_w = jax.random.normal(k2, (c // 2, hidden), dtype=jnp.float32) * 0.02
        fc2_b = jnp.zeros((c // 2,), dtype=jnp.float32)
        return {'x': x, 'fc1_w': fc1_w, 'fc1_b': fc1_b, 'fc2_w': fc2_w, 'fc2_b': fc2_b}
    _L0_ffn_all = _L0_ffn_setup()
    _L0_ffn_in = {k: v for k, v in _L0_ffn_all.items() if k in ('fc1_w', 'fc1_b', 'fc2_w', 'fc2_b')}
    del _L0_ffn_all
    return {'x': x, 'L0_tok_W': _L0_tok_in['W'], 'L0_tok_b': _L0_tok_in['b'], 'L0_tok_gamma': _L0_tok_in['gamma'], 'L0_tok_beta': _L0_tok_in['beta'], 'L0_ffn_fc1_w': _L0_ffn_in['fc1_w'], 'L0_ffn_fc1_b': _L0_ffn_in['fc1_b'], 'L0_ffn_fc2_w': _L0_ffn_in['fc2_w'], 'L0_ffn_fc2_b': _L0_ffn_in['fc2_b']}

def reference(x, L0_tok_W, L0_tok_b, L0_tok_gamma, L0_tok_beta, L0_ffn_fc1_w, L0_ffn_fc1_b, L0_ffn_fc2_w, L0_ffn_fc2_b):
    import jax
    import jax.numpy as jnp

    def _L0_tok_ref(x, W, b, gamma, beta):
        import jax, jax.numpy as jnp
        import numpy as np
        CTX = np.array([-2, -1, 0, 1, 2])
        STRIDE = 1
        EPS = 1e-05
        B, L, D = x.shape
        ctx = jnp.asarray(CTX)
        vi = jnp.arange(-int(CTX.min()), L - int(CTX.max()), STRIDE)
        idx = vi[:, None] + ctx[None, :]
        g = x[:, idx, :]
        g = g.reshape(B, vi.shape[0], -1)
        y = jnp.einsum('blk,ok->blo', g, W) + b
        y = jax.nn.relu(y)
        mean = jnp.mean(y, axis=(0, 1))
        var = jnp.var(y, axis=(0, 1))
        return (y - mean) * jax.lax.rsqrt(var + EPS) * gamma + beta

    def _L0_attn_ref(x):
        import jax, jax.numpy as jnp
        import numpy as np
        raw_weights = jnp.einsum('btk,bsk->bts', x, x)
        weights = jax.nn.softmax(raw_weights, axis=2)
        y = jnp.einsum('bts,bsk->btk', weights, x)
        return y

    def _L0_ffn_ref(x, fc1_w, fc1_b, fc2_w, fc2_b):
        import jax, jax.numpy as jnp
        import numpy as np

        def _haar_dwt2(x):
            a = x[:, ::2, ::2]
            b = x[:, ::2, 1::2]
            c = x[:, 1::2, ::2]
            d = x[:, 1::2, 1::2]
            ll = (a + b + c + d) * 0.5
            lh = (a + b - c - d) * 0.5
            hl = (a - b + c - d) * 0.5
            hh = (a - b - c + d) * 0.5
            return (ll, lh, hl, hh)

        def _haar_idwt2(ll, lh, hl, hh):
            a = (ll + lh + hl + hh) * 0.5
            b = (ll + lh - hl - hh) * 0.5
            c = (ll - lh + hl - hh) * 0.5
            d = (ll - lh - hl + hh) * 0.5
            B, H2, W2 = ll.shape
            out = jnp.zeros((B, 2 * H2, 2 * W2), ll.dtype)
            out = out.at[:, ::2, ::2].set(a)
            out = out.at[:, ::2, 1::2].set(b)
            out = out.at[:, 1::2, ::2].set(c)
            out = out.at[:, 1::2, 1::2].set(d)
            return out

        def _interp_linear_last(x, m):
            n = x.shape[-1]
            pos = jnp.linspace(0.0, 1.0, m, dtype=x.dtype) * (n - 1)
            i0 = jnp.clip(jnp.floor(pos).astype(jnp.int32), 0, n - 2)
            w = pos - i0.astype(x.dtype)
            return x[..., i0] * (1.0 - w) + x[..., i0 + 1] * w
        b, f, c = x.shape
        ll, lh, hl, hh = _haar_dwt2(x)
        ll_up = _interp_linear_last(ll, c)
        h = jax.nn.gelu(jnp.einsum('bfc,hc->bfh', ll_up, fc1_w) + fc1_b, approximate=False)
        ll_new = jnp.einsum('bfh,oh->bfo', h, fc2_w) + fc2_b
        return _haar_idwt2(ll_new, lh, hl, hh)
    h = _L0_tok_ref(x, L0_tok_W, L0_tok_b, L0_tok_gamma, L0_tok_beta)
    h = h + _L0_attn_ref(_layernorm(h, axis=-1))
    h = h + _L0_ffn_ref(_layernorm(h, axis=-1), L0_ffn_fc1_w, L0_ffn_fc1_b, L0_ffn_fc2_w, L0_ffn_fc2_b)
    return h

_drawn_inputs = setup_inputs


def setup_inputs(seed=0):
    import zlib

    import numpy as np

    out = dict(_drawn_inputs(seed))
    spreads = {'L0_tok_gamma': (1.0, 0.2),
     'L0_tok_beta': (0.0, 0.1),
     'L0_ffn_fc1_b': (0.0, 0.8),
     'L0_ffn_fc2_b': (0.0, 0.425)}
    factors = {'L0_tok_b': 8.0, 'L0_ffn_fc1_w': 7.437, 'L0_ffn_fc2_w': 6.547}
    for name, (base, spread) in spreads.items():
        noise = np.random.default_rng([zlib.crc32(name.encode()), seed]).standard_normal(out[name].shape)
        drawn = base * np.exp(spread * noise) if base else spread * noise
        out[name] = jnp.asarray(drawn.astype(out[name].dtype))
    for name, factor in factors.items():
        out[name] = (out[name] * factor).astype(out[name].dtype)
    return out
```

```python
import concourse.bass as bass
from concourse import mybir
from contextlib import ExitStack

FP32 = mybir.dt.float32
F32R = mybir.dt.float32r
FP16 = mybir.dt.float16
ALU = mybir.AluOpType
ACT = mybir.ActivationFunctionType

B, L, D = 8, 750, 80
TAPS = 5
C = 128
HID = 512
T = L - (TAPS - 1)
NP = T // 2
P = 128
EPS = 1e-5

NB = -(-NP // P)
NT = 2 * NB
ROWS = [min(P, NP - P * j) for j in range(NB)]
NPE = NP + 1
TPAD = NP + P * NB
ZW = 2 * NPE + P

PF = 2 * D
PB = PF - P
SPAN = 3
NPX = L // 2
XROWS = [min(P, NPX - P * j) for j in range(NB)]
XW = P + SPAN * PB
WPAD = D + P + SPAN * PF
X_DMAS = 2 * SPAN

KC = HID // P
CH = C // 2
SHIFT = -64.0


def tower_kernel(nc, x, tok_w, tok_b, tok_gamma, tok_beta, fc1_w, fc1_b, fc2_w, fc2_b, consts, out):
    ctx = ExitStack()
    with ctx:
        def sb(name, shape, dt=FP32):
            return ctx.enter_context(nc.sbuf_tensor(name, shape, dt))

        def ps(name, shape, dt=FP32):
            return ctx.enter_context(nc.psum_tensor(name, shape, dt))

        def sem(name):
            return ctx.enter_context(nc.semaphore(name))

        cst = sb("cst", [P, 3 * P])
        interp2, dup, ident = cst[:, 0:P], cst[:, P:2 * P], cst[:, 2 * P:3 * P]
        ident16 = sb("ident16", [P, P], FP16)
        wpad = sb("wpad", [P, WPAD])
        wb = sb("wb", [P, 2, SPAN, PB])
        bias_c = sb("bias_c", [P, 1])
        gamma_c = sb("gamma_c", [P, 1])
        beta_c = sb("beta_c", [P, 1])
        fc1_rows = sb("fc1_rows", [P, KC, C])
        fc1_bias = sb("fc1_bias", [P, KC])
        fc2_rows = sb("fc2_rows", [CH, HID])
        fc2_bias = sb("fc2_bias", [P, 1])
        shift_c = sb("shift_c", [P, 1])
        w_hi = sb("w_hi", [P, 2, SPAN + 1, C], F32R)
        w_lo = sb("w_lo", [P, 2, SPAN + 1, C], F32R)
        fc1_t = sb("fc1_t", [C, HID])
        fc1_hi = sb("fc1_hi", [P, HID], F32R)
        fc1_lo = sb("fc1_lo", [P, HID], F32R)
        fc2_hl = sb("fc2_hl", [P, KC, 2, CH], F32R)

        xin = [sb(f"xin{u}", [P, NB, XW]) for u in range(2)]
        xa_hi = [sb(f"xa_hi{u}", [P, NPX + 1], F32R) for u in range(2)]
        xa_lo = [sb(f"xa_lo{u}", [P, NPX + 1], F32R) for u in range(2)]
        xb_hi = [sb(f"xb_hi{u}", [SPAN * PB, NPE], F32R) for u in range(2)]
        xb_lo = [sb(f"xb_lo{u}", [SPAN * PB, NPE], F32R) for u in range(2)]
        y = sb("y", [C, (B - 1) * T + TPAD])
        bn = sb("bn", [C, 2 * B, 6])
        bn_mv = sb("bn_mv", [C, 2])
        bn_s = sb("bn_s", [C, 6])
        bn_scale = sb("bn_scale", [C, 1])
        bn_shift = sb("bn_shift", [C, 1])

        h_ch = sb("h_ch", [C, TPAD])
        h = [sb(f"h{u}", [P, NT, C]) for u in range(2)]
        z = [sb(f"z{u}", [P, NT, C + 1]) for u in range(2)]
        z_hi = sb("z_hi", [P, NT, C], FP16)
        z_lo = sb("z_lo", [P, NT, C], FP16)
        zt_hi = sb("zt_hi", [C, ZW], FP16)
        zt_lo = sb("zt_lo", [C, ZW], FP16)
        e = sb("e", [P, NT, TPAD])
        rden = sb("rden", [P, NT])
        h2 = sb("h2", [P, NT, C])
        n = sb("n", [P, NT, C])
        ln = sb("ln", [P, 2 * NT, 6])
        ln_sum = sb("ln_sum", [P, 2 * NT, 2])
        ln_dif = sb("ln_dif", [P, 2 * NT])
        ln_sq = sb("ln_sq", [P, 2 * NT])
        ln_var = sb("ln_var", [P, 2 * NT])
        ln_mean = sb("ln_mean", [P, 2 * NT])
        ln_log = sb("ln_log", [P, 2 * NT])
        ln_y = sb("ln_y", [P, 2 * NT])
        ln_y2 = sb("ln_y2", [P, 2 * NT])
        ln_y3 = sb("ln_y3", [P, 2 * NT])
        ln_rstd = sb("ln_rstd", [P, 2 * NT])
        q = sb("q", [P, NB, C])
        ll2 = sb("ll2", [P, NB, CH])
        ll_hl = sb("ll_hl", [P, NB, 2, CH], F32R)
        ll_t = sb("ll_t", [P, B, NPE], F32R)
        r = sb("r", [P, B, NT, C])

        g = [sb(f"g{u}", [P, KC, NPE]) for u in range(2)]
        g_hi = [sb(f"g_hi{u}", [P, KC, NPE], F32R) for u in range(2)]
        g_lo = [sb(f"g_lo{u}", [P, KC, NPE], F32R) for u in range(2)]
        u_sb = sb("u_sb", [P, NB * P])
        o = [sb(f"o{u}", [P, NB, 2, C]) for u in range(2)]

        bank03 = ps("bank03", [P, 4, 512])
        bank45 = ps("bank45", [P, 2, 512])
        bank67 = ps("bank67", [P, 2, 512])
        wt_ps = bank03[:, 0:2, :].rearrange("p a (g c) -> p a g c", c=C)
        fc1t_ps, fold_ps = bank03[:, 2, :], bank03[:, 3, :]
        fc2t_ps = bank03[:, 0, 0:KC * CH]
        xa_ps, xb_ps = bank67[:, 0, 0:NPX], bank67[0:SPAN * PB, 1, 0:NP]
        y_ps = bank45
        s_ps = bank03.rearrange("p (u a) n -> p u a n", u=2)
        o_ps = bank45
        h_ps = bank67.rearrange("p a n -> p (a n)")[:, 0:NT * C].rearrange("p (t c) -> p t c", c=C)
        zt_ps = bank67.bitcast(FP16)
        ll_ps = bank67[:, 0, 0:NPE]
        f_ps = bank03
        u_ps = bank45
        d_ps = bank67

        cst_in = sem("cst_in")
        w_in = sem("w_in")
        col_in = sem("col_in")
        fc_in = sem("fc_in")
        x_in = [sem(f"x_in{u}") for u in range(2)]
        out_done = [sem(f"out_done{u}") for u in range(2)]
        cleared = sem("cleared")
        ident16_ok = sem("ident16_ok")
        wb_ok = sem("wb_ok")
        wt_tr = sem("wt_tr")
        w_hi_ok, w_lo_ok = sem("w_hi_ok"), sem("w_lo_ok")
        x_tr = sem("x_tr")
        x_hi_ok, x_lo_ok = sem("x_hi_ok"), sem("x_lo_ok")
        y_mm = sem("y_mm")
        y_ok = sem("y_ok")
        y_st = sem("y_st")
        bn_step = sem("bn_step")
        bn_log = sem("bn_log")
        bn_y = sem("bn_y")
        bn_ok = sem("bn_ok")
        fct_tr = sem("fct_tr")
        fct_ok = sem("fct_ok")
        fold_mm = sem("fold_mm")
        fold_ok = sem("fold_ok")
        h_ch_ok = sem("h_ch_ok")
        h_tr = sem("h_tr")
        h_ok = sem("h_ok")
        st2_ok = sem("st2_ok")
        lnA, lnB, lnC = sem("lnA"), sem("lnB"), sem("lnC")
        ln_var_ok, ln_log_ok, ln_y_ok = sem("ln_var_ok"), sem("ln_log_ok"), sem("ln_y_ok")
        lnD, lnE, ln_ok = sem("lnD"), sem("lnE"), sem("ln_ok")
        z_ok, z_hi_ok, z_lo_ok = sem("z_ok"), sem("z_hi_ok"), sem("z_lo_ok")
        z_tr = sem("z_tr")
        zt_ok = sem("zt_ok")
        s_mm = sem("s_mm")
        e_ok = sem("e_ok")
        o_mm = sem("o_mm")
        rden_ok, h2_ok, n_ok = sem("rden_ok"), sem("h2_ok"), sem("n_ok")
        q_ok, ll2_ok, ll_hi_ok, ll_lo_ok = sem("q_ok"), sem("ll2_ok"), sem("ll_hi_ok"), sem("ll_lo_ok")
        r_ok = sem("r_ok")
        ll_tr = sem("ll_tr")
        ll_t_ok = sem("ll_t_ok")
        f_mm = sem("f_mm")
        g_ok, g_hi_ok, g_lo_ok = sem("g_ok"), sem("g_hi_ok"), sem("g_lo_ok")
        u_mm, u_ok, d_mm, o_ok = sem("u_mm"), sem("u_ok"), sem("d_mm"), sem("o_ok")

        block = ctx.enter_context(nc.Block())

        x_v = x.rearrange("b (p two) d -> b p (two d)", two=2)
        out_v = out.rearrange("b (p two) c -> b p (two c)", two=2)
        FULL = P * (NB - 1)

        def tile_cols(i):
            return (i // NB) * NP + (i % NB) * P

        @block.sync
        def _(sp):
            def load_x(b, u):
                for s in range(SPAN):
                    lo, w, at = (0, PF, 0) if s == 0 else (P, PB, P + s * PB)
                    last = (XROWS if s == 0 else ROWS)[-1]
                    sp.dma_start(xin[u][:, 0:NB - 1, at:at + w],
                                 x_v[b, s:s + FULL, lo:lo + w].rearrange("(j p) n -> p j n", p=P))\
                      .then_inc(x_in[u], 16)
                    sp.dma_start(xin[u][0:last, NB - 1, at:at + w],
                                 x_v[b, s + FULL:s + FULL + last, lo:lo + w]).then_inc(x_in[u], 16)

            sp.wait_ge(cleared, 1)
            sp.dma_start(wpad[:, D:D + TAPS * D], tok_w).then_inc(w_in, 16)
            sp.dma_start(cst[:, :], consts).then_inc(cst_in, 16)
            load_x(0, 0)
            load_x(1, 1)
            with sp.Fori(1, B // 2) as i:
                for u in range(2):
                    sp.wait_ge(x_tr, 2 * i + u - 1)
                    load_x(2 * i + u, u)

            def store(b, u, turn):
                sp.wait_ge(o_ok, b + 1)
                sp.dma_start(out_v[b, 0:FULL, :].rearrange("(j p) n -> p j n", p=P),
                             o[u][:, 0:NB - 1, :, :].rearrange("p j t c -> p j (t c)"))\
                  .then_inc(out_done[u], 16)
                sp.dma_start(out_v[b, FULL:NP, :],
                             o[u][0:ROWS[-1], NB - 1, :, :].rearrange("p t c -> p (t c)"))\
                  .then_inc(out_done[u], 16)

            with sp.Fori(0, B // 2) as i:
                for u in range(2):
                    store(2 * i + u, u, i)
            for u in range(2):
                sp.wait_ge(out_done[u], 32 * (B // 2))

        @block.gpsimd
        def _(pool):
            pool.memset(wpad[:, :], 0.0).then_inc(cleared, 1)
            pool.memset(fc2_bias[:, :], 0.0).then_inc(cleared, 1)
            pool.memset(shift_c[:, :], SHIFT).then_inc(cleared, 1)
            for u in range(2):
                pool.memset(xa_hi[u][:, NPX:NPX + 1].bitcast(FP32), 0.0)
                pool.memset(xa_lo[u][:, NPX:NPX + 1].bitcast(FP32), 0.0)
                pool.memset(xb_hi[u][:, NP:NPE].bitcast(FP32), 0.0)
                pool.memset(xb_lo[u][:, NP:NPE].bitcast(FP32), 0.0)
            pool.memset(y[:, B * T:], 0.0)
            pool.memset(zt_hi[:, 2 * NPE:], 0.0)
            pool.memset(zt_lo[:, 2 * NPE:], 0.0)
            pool.memset(e[:, :, T:], 1.0)
            pool.memset(u_sb[:, NPE:], 0.0).then_inc(r_ok, 1)
            for u in range(2):
                pool.memset(z[u][:, :, C:C + 1], 1.0).then_inc(cleared, 1)

            def residual(b):
                pool.wait_ge(n_ok, b + 1)
                pool.tensor_tensor(r[:, b, :, :].rearrange("p t c -> p (t c)"),
                                   h2[:, :, :].rearrange("p t c -> p (t c)"),
                                   n[:, :, :].rearrange("p t c -> p (t c)"), ALU.add).then_inc(r_ok, 1)

            with pool.Fori(0, B) as b:
                residual(b)

        @block.tensor
        def _(pe):
            pe.wait_ge(cst_in, 16)
            pe.wait_ge(w_in, 16)
            for par in range(2):
                off = D * (1 - par)
                for s in range(SPAN):
                    nc.tensor.transpose(wt_ps[:, par, s, :], wpad[:, off + PF * s:off + PF * s + P], ident)
            pe.wait_ge(wb_ok, 1)
            for par in range(2):
                last = nc.tensor.transpose(wt_ps[0:SPAN * PB, par, SPAN, :],
                                           wb[:, par, :, :].rearrange("p s n -> p (s n)"), ident)
            last.then_inc(wt_tr, 1)

            def transpose_x(b, u, turn):
                pe.wait_ge(x_in[u], 16 * X_DMAS * (turn + 1))
                if not (isinstance(b, int) and b == 0):
                    pe.wait_ge(x_lo_ok, b)
                for j in range(NB):
                    nc.tensor.transpose(xa_ps[:, P * j:P * j + XROWS[j]], xin[u][0:XROWS[j], j, 0:P],
                                        ident[0:XROWS[j], 0:XROWS[j]])
                for j in range(NB):
                    last = nc.tensor.transpose(xb_ps[:, P * j:P * j + ROWS[j]], xin[u][0:ROWS[j], j, P:XW],
                                               ident[0:ROWS[j], 0:ROWS[j]])
                last.then_inc(x_tr, 1)

            def context_products(b, u):
                pe.wait_ge(x_hi_ok, b + 1)
                pe.wait_ge(x_lo_ok, b + 1)
                for par in range(2):
                    if not (isinstance(b, int) and b == 0):
                        pe.wait_ge(y_ok, 2 * b - 1 + par)
                    k = 0
                    for s in range(SPAN + 1):
                        for w, xs in ((w_hi, (xa_hi, xb_hi)), (w_hi, (xa_lo, xb_lo)), (w_lo, (xa_hi, xb_hi))):
                            if s < SPAN:
                                lhs, rhs = w[:, par, s, :], xs[0][u][:, s:s + NPE]
                            else:
                                lhs, rhs = w[0:SPAN * PB, par, s, :], xs[1][u][:, :]
                            last = nc.tensor.matmul(y_ps[:, par, 0:NPE], lhs, rhs,
                                                    start=(k == 0), stop=(k == 3 * (SPAN + 1) - 1))
                            k += 1
                    last.then_inc(y_mm, 1)

            pe.wait_ge(cleared, 3)
            transpose_x(0, 0, 0)
            pe.wait_ge(w_hi_ok, 1)
            pe.wait_ge(w_lo_ok, 1)
            pe.wait_ge(cleared, 5)
            transpose_x(1, 1, 0)
            context_products(0, 0)
            with pe.Fori(0, B // 2 - 1) as i:
                transpose_x(2 * i + 2, 0, i + 1)
                context_products(2 * i + 1, 1)
                transpose_x(2 * i + 3, 1, i + 1)
                context_products(2 * i + 2, 0)
            context_products(B - 1, 1)

            pe.wait_ge(fc_in, 32)
            for k in range(KC):
                last = nc.tensor.transpose(fc1t_ps[:, P * k:P * k + P], fc1_rows[:, k, :], ident)
            last.then_inc(ll_tr, 1)
            for k in range(KC):
                last = nc.tensor.transpose(fc2t_ps[:, CH * k:CH * k + CH], fc2_rows[:, P * k:P * k + P],
                                           ident[0:CH, 0:CH])
            last.then_inc(fct_tr, 1)
            pe.wait_ge(fct_ok, 1)
            nc.tensor.matmul(fold_ps, interp2, fc1_t[:, :], start=True, stop=True).then_inc(fold_mm, 1)

            def transpose_h(b):
                pe.wait_ge(h_ch_ok, b + 1)
                if isinstance(b, int) and b == 0:
                    pe.wait_ge(x_lo_ok, B)
                else:
                    pe.wait_ge(zt_ok, 2 * b)
                for i in range(NT):
                    at = tile_cols(i)
                    last = nc.tensor.transpose(h_ps[:, i, :], h_ch[:, at:at + P], ident)
                last.then_inc(h_tr, 1)

            def transpose_z(b):
                pe.wait_ge(z_hi_ok, b + 1)
                for part, zs in enumerate((z_hi, z_lo)):
                    if part:
                        pe.wait_ge(z_lo_ok, b + 1)
                    for i in range(NT):
                        par, j = i // NB, i % NB
                        rows = min(P, NPE - P * j)
                        at = par * NPE + P * j
                        last = nc.tensor.transpose(zt_ps[:, part, at:at + rows], zs[0:rows, i, :],
                                                   ident16[0:rows, 0:rows])
                    last.then_inc(z_tr, 1)

            def transpose_ll(b):
                pe.wait_ge(ll_lo_ok, b + 1)
                for j in range(NB):
                    rows = min(P, NPE - P * j)
                    last = nc.tensor.transpose(ll_ps[:, P * j:P * j + rows],
                                               ll_hl[0:rows, j, :, :].rearrange("p a c -> p (a c)").bitcast(FP32),
                                               ident[0:rows, 0:rows])
                last.then_inc(ll_tr, 1)

            def scores(b, i):
                at = (i // NB) * NPE + (i % NB) * P
                if not (isinstance(b, int) and b == 0 and i < 2):
                    pe.wait_ge(e_ok, NT * b + i - 1)
                for par in range(2):
                    cols = slice(par * NPE, par * NPE + NP)
                    dst = s_ps[:, i % 2, par, 0:NP]
                    nc.tensor.matmul(dst, zt_hi[:, at:at + P], zt_hi[:, cols], start=True, stop=False)
                    nc.tensor.matmul(dst, zt_hi[:, at:at + P], zt_lo[:, cols], start=False, stop=False)
                    last = nc.tensor.matmul(dst, zt_lo[:, at:at + P], zt_hi[:, cols], start=False, stop=True)
                last.then_inc(s_mm, 1)

            def attend(b, zu, i):
                par, j = i // NB, i % NB
                if j == 0:
                    if isinstance(b, int) and b == 0:
                        pe.wait_ge(y_ok, 2 * B)
                    else:
                        pe.wait_ge(h2_ok, 2 * b - 1 + par)
                for k in range(NT):
                    if i == 0:
                        pe.wait_ge(e_ok, NT * b + k + 1)
                    rows = ROWS[k % NB]
                    last = nc.tensor.matmul(o_ps[:, par, j * (C + 1):(j + 1) * (C + 1)],
                                            e[0:rows, k, tile_cols(i):tile_cols(i) + P],
                                            z[zu][0:rows, k, :], start=(k == 0), stop=(k == NT - 1))
                if j == NB - 1:
                    last.then_inc(o_mm, 1)

            def attention(b, u, first=False, last=False):
                pe.wait_ge(zt_ok, 2 * b + 2)
                scores(b, 0)
                scores(b, 1)
                if not last:
                    transpose_h(b + 1)
                for i in range(2, NT):
                    scores(b, i)
                attend(b, u, 0)
                attend(b, u, 1)
                if not first:
                    pe.wait_ge(h_ok, B if last else b + 2)
                    transpose_ll(b - 1)
                attend(b, u, 2)
                attend(b, u, 3)
                if not last:
                    if not first:
                        pe.wait_ge(ll_t_ok, b)
                    else:
                        pe.wait_ge(h_ok, b + 2)
                    transpose_z(b + 1)
                attend(b, u, 4)
                attend(b, u, 5)

            pe.wait_ge(ident16_ok, 1)
            transpose_h(0)
            pe.wait_ge(h_ok, 1)
            transpose_z(0)
            pe.wait_ge(fold_ok, 1)
            attention(0, 0, first=True)
            with pe.Fori(0, B // 2 - 1) as i:
                attention(2 * i + 1, 1)
                attention(2 * i + 2, 0)
            attention(B - 1, 1, last=True)

            def hidden(b, u):
                for k in range(KC):
                    if isinstance(b, int) and b == 0:
                        pe.wait_ge(e_ok, B * NT)
                    else:
                        pe.wait_ge(g_ok, KC * b - (KC - 1) + k)
                    rhs = ll_t[:, b, :]
                    nc.tensor.matmul(f_ps[:, k, 0:NPE], fc1_hi[:, P * k:P * k + P], rhs, start=True, stop=False)
                    nc.tensor.matmul(f_ps[:, k, 0:NPE], fc1_lo[:, P * k:P * k + P], rhs, start=False, stop=True)\
                      .then_inc(f_mm, 1)

            def project(b, u):
                if isinstance(b, int) and b < 2:
                    pe.wait_ge(h2_ok, 2 * B)
                else:
                    pe.wait_ge(u_ok, b - 1)
                for k in range(KC):
                    pe.wait_ge(g_hi_ok, KC * b + k + 1)
                    lhs = fc2_hl[:, k, :, :].rearrange("p a c -> p (a c)")
                    nc.tensor.matmul(u_ps[:, u, 0:NPE], lhs, g_hi[u][:, k, :], start=(k == 0), stop=False)
                    pe.wait_ge(g_lo_ok, KC * b + k + 1)
                    last = nc.tensor.matmul(u_ps[:, u, 0:NPE], lhs, g_lo[u][:, k, :], start=False, stop=(k == KC - 1))
                last.then_inc(u_mm, 1)

            def spread(b, u):
                pe.wait_ge(u_ok, b + 1)
                if isinstance(b, int) and b < 2:
                    pe.wait_ge(ll_t_ok, B)
                else:
                    pe.wait_ge(o_ok, b - 1)
                for j in range(NB):
                    last = nc.tensor.matmul(d_ps[:, u, C * j:C * j + C], u_sb[:, P * j:P * j + P], dup,
                                            start=True, stop=True)
                last.then_inc(d_mm, 1)

            hidden(0, 0)
            pe.wait_ge(h_ok, B)
            transpose_ll(B - 1)
            hidden(1, 1)
            project(0, 0)
            for b in (2, 3):
                hidden(b, b % 2)
                spread(b - 2, b % 2)
                project(b - 1, 1 - b % 2)
            with pe.Fori(2, B // 2) as i:
                for u in range(2):
                    hidden(2 * i + u, u)
                    spread(2 * i + u - 2, u)
                    project(2 * i + u - 1, 1 - u)
            spread(B - 2, 0)
            project(B - 1, 1)
            spread(B - 1, 1)

        @block.scalar
        def _(act):
            act.dma_start(bias_c[:, :], tok_b.rearrange("(p a) -> p a", a=1)).then_inc(col_in, 16)
            act.dma_start(gamma_c[:, :], tok_gamma.rearrange("(p a) -> p a", a=1)).then_inc(col_in, 16)
            act.dma_start(beta_c[:, :], tok_beta.rearrange("(p a) -> p a", a=1)).then_inc(col_in, 16)
            for k in range(KC):
                act.dma_start(fc1_bias[:, k:k + 1], fc1_b[P * k:P * k + P].rearrange("(p a) -> p a", a=1))\
                   .then_inc(col_in, 16)
            act.wait_ge(cleared, 3)
            act.dma_start(fc2_bias[0:CH, :], fc2_b.rearrange("(p a) -> p a", a=1)).then_inc(col_in, 16)
            act.dma_start(fc1_rows[:, :, :], fc1_w.rearrange("(k p) c -> p k c", p=P)).then_inc(fc_in, 16)
            act.dma_start(fc2_rows[:, :], fc2_w).then_inc(fc_in, 16)
            act.wait_ge(cst_in, 16)
            nc.scalar.activation(ident16[:, :], ident, ACT.Copy).then_inc(ident16_ok, 1)
            act.wait_ge(wt_tr, 1)
            nc.scalar.activation(w_hi[:, :, 0:SPAN, :], wt_ps[:, :, 0:SPAN, :], ACT.Copy)
            nc.scalar.activation(w_hi[0:SPAN * PB, :, SPAN, :], wt_ps[0:SPAN * PB, :, SPAN, :], ACT.Copy)\
              .then_inc(w_hi_ok, 1)

            def frames_hi(b, u):
                act.wait_ge(x_tr, b + 1)
                if not (isinstance(b, int) and b < 2):
                    act.wait_ge(y_mm, 2 * b - 2)
                nc.scalar.activation(xa_hi[u][:, 0:NPX], xa_ps, ACT.Copy)
                nc.scalar.activation(xb_hi[u][:, 0:NP], xb_ps, ACT.Copy).then_inc(x_hi_ok, 1)

            def relu(b):
                for par in range(2):
                    act.wait_ge(y_mm, 2 * b + par + 1)
                    nc.scalar.activation(y[:, bass.ds(b * T + par * NP, NP)], y_ps[:, par, 0:NP], ACT.Relu,
                                         bias=bias_c[:, :]).then_inc(y_ok, 1)

            frames_hi(0, 0)
            act.wait_ge(col_in, 16 * (4 + KC))
            frames_hi(1, 1)
            relu(0)
            with act.Fori(0, B // 2 - 1) as i:
                frames_hi(2 * i + 2, 0)
                relu(2 * i + 1)
                frames_hi(2 * i + 3, 1)
                relu(2 * i + 2)
            relu(B - 1)

            act.wait_ge(bn_step, 2)
            nc.scalar.activation(bn_s[:, 1:2], bn_s[:, 0:1], ACT.Ln).then_inc(bn_log, 1)
            act.wait_ge(bn_log, 1)
            nc.scalar.activation(bn_s[:, 2:3], bn_s[:, 1:2], ACT.Exp, scale=-0.5).then_inc(bn_y, 1)

            def normalise_channels(b):
                if isinstance(b, int) and b == 0:
                    act.wait_ge(bn_ok, 2)
                else:
                    act.wait_ge(h_tr, b)
                nc.scalar.activation(h_ch[:, :], y[:, bass.ds(b * T, TPAD)], ACT.Identity,
                                     bias=bn_shift[:, :], scale=bn_scale[:, :]).then_inc(h_ch_ok, 1)

            def copy_h(b, u):
                act.wait_ge(h_tr, b + 1)
                if not (isinstance(b, int) and b < 2):
                    act.wait_ge(h2_ok, 2 * b - 2)
                nc.scalar.activation(h[u][:, :, :], h_ps, ACT.Copy).then_inc(h_ok, 1)

            def rsqrt(lo, hi, turn):
                act.wait_ge(ln_var_ok, turn)
                nc.scalar.activation(ln_log[:, lo:hi], ln_var[:, lo:hi], ACT.Ln, scale=1.0 / C)\
                  .then_inc(ln_log_ok, 1)
                act.wait_ge(ln_log_ok, turn)
                nc.scalar.activation(ln_y[:, lo:hi], ln_log[:, lo:hi], ACT.Exp, scale=-0.5)\
                  .then_inc(ln_y_ok, 1)

            def exponentials(b, i):
                act.wait_ge(s_mm, NT * b + i + 1)
                if i == 0 and not (isinstance(b, int) and b == 0):
                    act.wait_ge(o_mm, 2 * b)
                nc.scalar.activation(e[:, i, 0:T].rearrange("p (a n) -> p a n", a=2), s_ps[:, i % 2, :, 0:NP],
                                     ACT.Exp, bias=shift_c[:, :]).then_inc(e_ok, 1)

            def copy_ll(b):
                act.wait_ge(ll_tr, b + 2)
                nc.scalar.activation(ll_t[:, b, :], ll_ps, ACT.Copy).then_inc(ll_t_ok, 1)

            def attention(b, u, first=False, last=False):
                exponentials(b, 0)
                exponentials(b, 1)
                if not last:
                    copy_h(b + 1, 1 - u)
                for i in range(2, 5):
                    exponentials(b, i)
                rsqrt(NT if first else 0, NT if last else 2 * NT, b + 2)
                exponentials(b, 5)
                if not last and not (isinstance(b, int) and b == B - 2):
                    normalise_channels(b + 2)
                if not first:
                    copy_ll(b - 1)

            normalise_channels(0)
            copy_h(0, 0)
            normalise_channels(1)
            rsqrt(NT, 2 * NT, 1)
            attention(0, 0, first=True)
            with act.Fori(0, B // 2 - 2) as i:
                attention(2 * i + 1, 1)
                attention(2 * i + 2, 0)
            attention(B - 3, 1)
            attention(B - 2, 0)
            attention(B - 1, 1, last=True)
            rsqrt(0, NT, B + 2)

            def gelu(b, u):
                for k in range(KC):
                    act.wait_ge(f_mm, KC * b + k + 1)
                    if k == 0 and not (isinstance(b, int) and b < 2):
                        act.wait_ge(g_lo_ok, KC * b - KC)
                    nc.scalar.activation(g[u][:, k, :], f_ps[:, k, 0:NPE], ACT.Gelu,
                                         bias=fc1_bias[:, k:k + 1]).then_inc(g_ok, 1)

            gelu(0, 0)
            copy_ll(B - 1)
            gelu(1, 1)
            with act.Fori(1, B // 2) as i:
                for u in range(2):
                    gelu(2 * i + u, u)

        @block.vector
        def _(dve):
            dve.wait_ge(w_in, 16)
            for par in range(2):
                at = D * (1 - par) + P
                last = nc.vector.tensor_copy(
                    wb[:, par, :, :], wpad[:, at:at + SPAN * PF].rearrange("p (s n) -> p s n", n=PF)[:, :, 0:PB])
            last.then_inc(wb_ok, 1)
            dve.wait_ge(w_hi_ok, 1)
            nc.vector.tensor_tensor(w_lo[:, :, 0:SPAN, :], wt_ps[:, :, 0:SPAN, :],
                                    w_hi[:, :, 0:SPAN, :].bitcast(FP32), ALU.subtract)
            nc.vector.tensor_tensor(w_lo[0:SPAN * PB, :, SPAN, :], wt_ps[0:SPAN * PB, :, SPAN, :],
                                    w_hi[0:SPAN * PB, :, SPAN, :].bitcast(FP32), ALU.subtract)\
              .then_inc(w_lo_ok, 1)

            def frames_lo(b, u):
                dve.wait_ge(x_hi_ok, b + 1)
                nc.vector.tensor_tensor(xa_lo[u][:, 0:NPX], xa_ps, xa_hi[u][:, 0:NPX].bitcast(FP32), ALU.subtract)
                nc.vector.tensor_tensor(xb_lo[u][:, 0:NP], xb_ps, xb_hi[u][:, 0:NP].bitcast(FP32), ALU.subtract)\
                  .then_inc(x_lo_ok, 1)

            def channel_stats(b):
                for par in range(2):
                    dve.wait_ge(y_ok, 2 * b + par + 1)
                    nc.vector.bn_stats(bn[:, bass.ds(2 * b + par, 1), :].rearrange("p a s -> p (a s)"),
                                       y[:, bass.ds(b * T + par * NP, NP)]).then_inc(y_st, 1)

            frames_lo(0, 0)
            frames_lo(1, 1)
            channel_stats(0)
            with dve.Fori(0, B // 2 - 1) as i:
                frames_lo(2 * i + 2, 0)
                channel_stats(2 * i + 1)
                frames_lo(2 * i + 3, 1)
                channel_stats(2 * i + 2)
            channel_stats(B - 1)

            dve.wait_ge(y_st, 2 * B)
            nc.vector.bn_aggr(bn_mv[:, :], bn[:, :, :].rearrange("p a s -> p (a s)")).then_inc(bn_step, 1)
            dve.wait_ge(bn_step, 1)
            nc.vector.tensor_scalar_add(bn_s[:, 0:1], bn_mv[:, 1:2], EPS).then_inc(bn_step, 1)
            dve.wait_ge(bn_y, 1)
            dve.wait_ge(bn_step, 2)
            nc.vector.tensor_tensor(bn_s[:, 3:4], bn_s[:, 2:3], bn_s[:, 2:3], ALU.mult).then_inc(bn_step, 1)
            dve.wait_ge(bn_step, 3)
            nc.vector.scalar_tensor_tensor(bn_s[:, 4:5], bn_s[:, 3:4], -0.5, bn_s[:, 0:1], ALU.mult, ALU.mult)\
              .then_inc(bn_step, 1)
            dve.wait_ge(bn_step, 4)
            nc.vector.scalar_tensor_tensor(bn_s[:, 5:6], bn_s[:, 4:5], 1.5, bn_s[:, 2:3], ALU.add, ALU.mult)\
              .then_inc(bn_step, 1)
            dve.wait_ge(bn_step, 5)
            nc.vector.tensor_tensor(bn_scale[:, :], bn_s[:, 5:6], gamma_c[:, :], ALU.mult).then_inc(bn_ok, 1)
            dve.wait_ge(bn_ok, 1)
            nc.vector.tensor_tensor(bn_s[:, 3:4], bn_mv[:, 0:1], bn_scale[:, :], ALU.mult).then_inc(bn_step, 1)
            dve.wait_ge(bn_step, 6)
            nc.vector.tensor_tensor(bn_shift[:, :], beta_c[:, :], bn_s[:, 3:4], ALU.subtract).then_inc(bn_ok, 1)

            dve.wait_ge(fct_tr, 1)
            nc.vector.tensor_copy(fc1_t[:, :], fc1t_ps).then_inc(fct_ok, 1)
            fc2t = fc2t_ps.rearrange("p (k c) -> p k c", c=CH)
            nc.vector.tensor_copy(fc2_hl[:, :, 0, :], fc2t).then_inc(fct_ok, 1)
            dve.wait_ge(fct_ok, 2)
            nc.vector.tensor_tensor(fc2_hl[:, :, 1, :], fc2t, fc2_hl[:, :, 0, :].bitcast(FP32), ALU.subtract)
            dve.wait_ge(fold_mm, 1)
            nc.vector.tensor_copy(fc1_hi[:, :], fold_ps).then_inc(fct_ok, 1)
            dve.wait_ge(fct_ok, 3)
            nc.vector.tensor_tensor(fc1_lo[:, :], fold_ps, fc1_hi[:, :].bitcast(FP32), ALU.subtract)\
              .then_inc(fold_ok, 1)

            def add_attention(b, u):
                for par in range(2):
                    dve.wait_ge(o_mm, 2 * b + par + 1)
                    ov = o_ps[:, par, 0:NB * (C + 1)].rearrange("p (j c) -> p j c", c=C + 1)
                    nc.vector.reciprocal(rden[:, NB * par:NB * par + NB], ov[:, :, C]).then_inc(rden_ok, 1)
                    dve.wait_ge(rden_ok, 2 * b + par + 1)
                    if par == 0:
                        dve.wait_ge(r_ok, b + 1)
                    for j in range(NB):
                        i = NB * par + j
                        last = nc.vector.scalar_tensor_tensor(h2[:, i, :], ov[:, j, 0:C], rden[:, i:i + 1],
                                                              h[u][:, i, :], ALU.mult, ALU.add)
                    last.then_inc(h2_ok, 1)
                dve.wait_ge(h2_ok, 2 * b + 2)
                for i in range(NT):
                    last = nc.vector.bn_stats(ln[:, i, :], h2[:, i, :])
                last.then_inc(st2_ok, 1)

            def first_stats(b, u):
                dve.wait_ge(h_ok, b + 1)
                for i in range(NT):
                    last = nc.vector.bn_stats(ln[:, NT + i, :], h[u][:, i, :])
                last.then_inc(st2_ok, 1)

            def variances(lo, hi, turn, stats):
                dve.wait_ge(st2_ok, stats)
                nc.vector.tensor_tensor(ln_sum[:, lo:hi, :], ln[:, lo:hi, 1:3], ln[:, lo:hi, 4:6], ALU.add)\
                  .then_inc(lnA, 1)
                nc.vector.tensor_tensor(ln_dif[:, lo:hi], ln[:, lo:hi, 1], ln[:, lo:hi, 4], ALU.subtract)\
                  .then_inc(lnB, 1)
                dve.wait_ge(lnB, turn)
                nc.vector.scalar_tensor_tensor(ln_sq[:, lo:hi], ln_dif[:, lo:hi], C / 4.0, ln_dif[:, lo:hi],
                                               ALU.mult, ALU.mult).then_inc(lnC, 1)
                dve.wait_ge(lnA, turn)
                nc.vector.tensor_scalar(ln_mean[:, lo:hi], ln_sum[:, lo:hi, 0], 0.5, None, ALU.mult)
                dve.wait_ge(lnC, turn)
                nc.vector.scalar_tensor_tensor(ln_var[:, lo:hi], ln_sq[:, lo:hi], C * EPS, ln_sum[:, lo:hi, 1],
                                               ALU.add, ALU.add).then_inc(ln_var_ok, 1)

            def newton(lo, hi, turn):
                dve.wait_ge(ln_y_ok, turn)
                dve.wait_ge(ln_var_ok, turn)
                nc.vector.tensor_tensor(ln_y2[:, lo:hi], ln_y[:, lo:hi], ln_y[:, lo:hi], ALU.mult).then_inc(lnD, 1)
                dve.wait_ge(lnD, turn)
                nc.vector.scalar_tensor_tensor(ln_y3[:, lo:hi], ln_y2[:, lo:hi], -0.5 / C, ln_var[:, lo:hi],
                                               ALU.mult, ALU.mult).then_inc(lnE, 1)
                dve.wait_ge(lnE, turn)
                nc.vector.scalar_tensor_tensor(ln_rstd[:, lo:hi], ln_y3[:, lo:hi], 1.5, ln_y[:, lo:hi],
                                               ALU.add, ALU.mult).then_inc(ln_ok, 1)
                dve.wait_ge(ln_ok, turn)

            def band(b):
                for i in range(NT):
                    last = nc.vector.tensor_scalar(n[:, i, :], h2[:, i, :], ln_mean[:, i:i + 1],
                                                   ln_rstd[:, i:i + 1], ALU.subtract, ALU.mult)
                last.then_inc(n_ok, 1)
                dve.wait_ge(n_ok, b + 1)
                nc.vector.tensor_tensor(q[:, :, :], n[:, 0:NB, :], n[:, NB:NT, :], ALU.add).then_inc(q_ok, 1)
                dve.wait_ge(q_ok, b + 1)
                qv = q[:, :, :].rearrange("p j (c two) -> p j c two", two=2)
                nc.vector.tensor_tensor(ll2[:, :, :], qv[:, :, :, 0], qv[:, :, :, 1], ALU.add).then_inc(ll2_ok, 1)
                dve.wait_ge(ll2_ok, b + 1)
                dve.wait_ge(ll_tr, b + 1)
                nc.vector.tensor_scalar(ll_hl[:, :, 0, :], ll2[:, :, :], 0.5, None, ALU.mult).then_inc(ll_hi_ok, 1)
                dve.wait_ge(ll_hi_ok, b + 1)
                nc.vector.scalar_tensor_tensor(ll_hl[:, :, 1, :], ll2[:, :, :], 0.5,
                                               ll_hl[:, :, 0, :].bitcast(FP32), ALU.mult, ALU.subtract)\
                  .then_inc(ll_lo_ok, 1)

            def first_norm(b, u):
                if not (isinstance(b, int) and b < 2):
                    dve.wait_ge(o_mm, 2 * b - 2)
                for i in range(NT):
                    last = nc.vector.tensor_scalar(z[u][:, i, 0:C], h[u][:, i, :], ln_mean[:, NT + i:NT + i + 1],
                                                   ln_rstd[:, NT + i:NT + i + 1], ALU.subtract, ALU.mult)
                last.then_inc(z_ok, 1)
                dve.wait_ge(z_ok, b + 1)
                if not (isinstance(b, int) and b == 0):
                    dve.wait_ge(z_tr, 2 * b)
                nc.vector.tensor_copy(z_hi[:, :, :], z[u][:, :, 0:C]).then_inc(z_hi_ok, 1)
                dve.wait_ge(z_hi_ok, b + 1)
                nc.vector.tensor_tensor(z_lo[:, :, :], z[u][:, :, 0:C], z_hi[:, :, :], ALU.subtract)\
                  .then_inc(z_lo_ok, 1)

            def copy_zt(b):
                if not (isinstance(b, int) and b == 0):
                    dve.wait_ge(s_mm, NT * b)
                dve.wait_ge(z_tr, 2 * b + 1)
                nc.vector.tensor_copy(zt_hi[:, 0:2 * NPE], zt_ps[:, 0, 0:2 * NPE]).then_inc(zt_ok, 1)
                dve.wait_ge(z_tr, 2 * b + 2)
                nc.vector.tensor_copy(zt_lo[:, 0:2 * NPE], zt_ps[:, 1, 0:2 * NPE]).then_inc(zt_ok, 1)

            def attention(b, u, first=False, last=False):
                if not first:
                    add_attention(b - 1, 1 - u)
                if not last:
                    first_stats(b + 1, 1 - u)
                lo, hi = NT if first else 0, NT if last else 2 * NT
                variances(lo, hi, b + 2, 2 * b + 2 if not last else 2 * B - 1)
                newton(lo, hi, b + 2)
                if not first:
                    band(b - 1)
                if not last:
                    first_norm(b + 1, 1 - u)
                    copy_zt(b + 1)

            first_stats(0, 0)
            variances(NT, 2 * NT, 1, 1)
            newton(NT, 2 * NT, 1)
            first_norm(0, 0)
            copy_zt(0)
            attention(0, 0, first=True)
            with dve.Fori(0, B // 2 - 1) as i:
                attention(2 * i + 1, 1)
                attention(2 * i + 2, 0)
            attention(B - 1, 1, last=True)
            add_attention(B - 1, 1)
            variances(0, NT, B + 2, 2 * B)
            newton(0, NT, B + 2)
            band(B - 1)

            def split_g(b, u):
                for k in range(KC):
                    dve.wait_ge(g_ok, KC * b + k + 1)
                    if k == 0 and not (isinstance(b, int) and b < 2):
                        dve.wait_ge(u_mm, b - 1)
                    nc.vector.tensor_copy(g_hi[u][:, k, :], g[u][:, k, :]).then_inc(g_hi_ok, 1)
                    dve.wait_ge(g_hi_ok, KC * b + k + 1)
                    nc.vector.tensor_tensor(g_lo[u][:, k, :], g[u][:, k, :], g_hi[u][:, k, :].bitcast(FP32),
                                            ALU.subtract).then_inc(g_lo_ok, 1)

            def band_change(b, u):
                dve.wait_ge(u_mm, b + 1)
                if not (isinstance(b, int) and b == 0):
                    dve.wait_ge(d_mm, b)
                dve.wait_ge(ll_t_ok, b + 1)
                nc.vector.scalar_tensor_tensor(u_sb[:, 0:NPE], u_ps[:, u, 0:NPE], fc2_bias[:, :],
                                               ll_t[:, b, :].bitcast(FP32), ALU.add, ALU.subtract)\
                  .then_inc(u_ok, 1)

            def finish(b, u, turn):
                dve.wait_ge(d_mm, b + 1)
                dve.wait_ge(r_ok, b + 2)
                if not (isinstance(b, int) and b < 2):
                    dve.wait_ge(out_done[u], 32 * turn)
                dv = d_ps[:, u, 0:NB * C].rearrange("p (j c) -> p j c", c=C)
                rv = r[:, b, :, :]
                for par in range(2):
                    last = nc.vector.tensor_tensor(o[u][:, :, par, :], dv, rv[:, NB * par:NB * par + NB, :],
                                                   ALU.add)
                last.then_inc(o_ok, 1)

            split_g(0, 0)
            split_g(1, 1)
            band_change(0, 0)
            split_g(2, 0)
            band_change(1, 1)
            finish(0, 0, 0)
            split_g(3, 1)
            band_change(2, 0)
            finish(1, 1, 0)
            with dve.Fori(2, B // 2) as i:
                split_g(2 * i, 0)
                band_change(2 * i - 1, 1)
                finish(2 * i - 2, 0, i - 1)
                split_g(2 * i + 1, 1)
                band_change(2 * i, 0)
                finish(2 * i - 1, 1, i - 1)
            band_change(B - 1, 1)
            finish(B - 2, 0, B // 2 - 1)
            finish(B - 1, 1, B // 2 - 1)


_INS = ['x', 'L0_tok_W', 'L0_tok_b', 'L0_tok_gamma', 'L0_tok_beta', 'L0_ffn_fc1_w', 'L0_ffn_fc1_b',
        'L0_ffn_fc2_w', 'L0_ffn_fc2_b']


def _shape_constants():
    import numpy as np
    pos = np.linspace(0.0, 1.0, C, dtype=np.float32) * np.float32(CH - 1)
    i0 = np.clip(np.floor(pos).astype(np.int32), 0, CH - 2)
    w = pos - i0.astype(np.float32)
    a = np.zeros((C, CH), np.float32)
    a[np.arange(C), i0] += np.float32(1.0) - w
    a[np.arange(C), i0 + 1] += w
    half = np.zeros((CH, C), np.float32)
    half[np.arange(C) // 2, np.arange(C)] = 0.5
    return np.concatenate([a, a, np.concatenate([half, half], 0), np.eye(P, dtype=np.float32)], 1)


def kernel(**inputs):
    import numpy as _np
    import concourse.bacc as _bacc
    from concourse import mybir as _mybir
    from concourse.bass_utils import run_bass_kernel_spmd as _run

    nc = _bacc.Bacc("TRN2", target_bir_lowering=False, num_devices=1)
    arrays, args = {}, []
    for name in _INS:
        arrays[f"in_{name}"] = _np.ascontiguousarray(inputs[name])
    arrays["in_consts"] = _shape_constants()
    for name, a in arrays.items():
        args.append(nc.dram_tensor(name, a.shape, _mybir.dt.from_np(a.dtype), kind="ExternalInput").ap())
    args.append(nc.dram_tensor("out", (B, T, C), _mybir.dt.float32, kind="ExternalOutput").ap())
    tower_kernel(nc, *args)
    r = _run(nc, [arrays], core_ids=[0])
    return r.results[0]["out"]
```

```python
import concourse.bass as bass
from concourse import mybir
from contextlib import ExitStack

FP32 = mybir.dt.float32
F32R = mybir.dt.float32r
FP16 = mybir.dt.float16
ALU = mybir.AluOpType
ACT = mybir.ActivationFunctionType

B, L, D = 8, 750, 80
TAPS = 5
C = 128
HID = 512
T = L - (TAPS - 1)
NP = T // 2
P = 128
EPS = 1e-5

NB = -(-NP // P)
NT = 2 * NB
ROWS = [min(P, NP - P * j) for j in range(NB)]
NPE = NP + 1
TPAD = NP + P * NB
ZW = 2 * NPE + P

PF = 2 * D
PB = PF - P
SPAN = 3
NPX = L // 2
XROWS = [min(P, NPX - P * j) for j in range(NB)]
XW = P + SPAN * PB
WPAD = D + P + SPAN * PF
X_DMAS = 2 * SPAN

KC = HID // P
CH = C // 2
RSQRT_STEPS = 11
LN_STEPS = 5 + RSQRT_STEPS
SHIFT = -64.0


def tower_kernel(nc, x, tok_w, tok_b, tok_gamma, tok_beta, fc1_w, fc1_b, fc2_w, fc2_b, consts, out):
    ctx = ExitStack()
    with ctx:
        def sb(name, shape, dt=FP32):
            return ctx.enter_context(nc.sbuf_tensor(name, shape, dt))

        def ps(name, shape, dt=FP32):
            return ctx.enter_context(nc.psum_tensor(name, shape, dt))

        def sem(name):
            return ctx.enter_context(nc.semaphore(name))

        cst = sb("cst", [P, 3 * P])
        interp2, dup, ident = cst[:, 0:P], cst[:, P:2 * P], cst[:, 2 * P:3 * P]
        ident16 = sb("ident16", [P, P], FP16)
        wpad = sb("wpad", [P, WPAD])
        wb = sb("wb", [P, 2, SPAN, PB])
        bias_c = sb("bias_c", [P, 1])
        gamma_c = sb("gamma_c", [P, 1])
        beta_c = sb("beta_c", [P, 1])
        fc1_rows = sb("fc1_rows", [P, KC, C])
        fc1_bias = sb("fc1_bias", [P, KC])
        fc2_rows = sb("fc2_rows", [CH, HID])
        fc2_bias = sb("fc2_bias", [P, 1])
        shift_c = sb("shift_c", [P, 1])
        w_hi = sb("w_hi", [P, 2, SPAN + 1, C], F32R)
        w_lo = sb("w_lo", [P, 2, SPAN + 1, C], F32R)
        fc1_t = sb("fc1_t", [C, HID])
        fc1_hi = sb("fc1_hi", [P, HID], F32R)
        fc1_lo = sb("fc1_lo", [P, HID], F32R)
        fc2_hl = sb("fc2_hl", [P, KC, 2, CH], F32R)

        xin = [sb(f"xin{u}", [P, NB, XW]) for u in range(2)]
        xa_hi = [sb(f"xa_hi{u}", [P, NPX + 1], F32R) for u in range(2)]
        xa_lo = [sb(f"xa_lo{u}", [P, NPX + 1], F32R) for u in range(2)]
        xb_hi = [sb(f"xb_hi{u}", [SPAN * PB, NPE], F32R) for u in range(2)]
        xb_lo = [sb(f"xb_lo{u}", [SPAN * PB, NPE], F32R) for u in range(2)]
        y = sb("y", [C, (B - 1) * T + TPAD])
        bn = sb("bn", [C, 2 * B, 6])
        bn_mv = sb("bn_mv", [C, 2])
        bn_var = sb("bn_var", [C, 1])
        bn_y = sb("bn_y", [C, 8])
        bn_off = sb("bn_off", [C, 1])
        bn_scale = sb("bn_scale", [C, 1])
        bn_shift = sb("bn_shift", [C, 1])

        h_ch = sb("h_ch", [C, TPAD])
        h = [sb(f"h{u}", [P, NT, C]) for u in range(2)]
        z = [sb(f"z{u}", [P, NT, C + 1]) for u in range(2)]
        z_hi = sb("z_hi", [P, NT, C], FP16)
        z_lo = sb("z_lo", [P, NT, C], FP16)
        zt_hi = sb("zt_hi", [C, ZW], FP16)
        zt_lo = sb("zt_lo", [C, ZW], FP16)
        e = sb("e", [P, NT, TPAD])
        rden = sb("rden", [P, NT])
        h2 = sb("h2", [P, NT, C])
        n = sb("n", [P, NT, C])
        ln = sb("ln", [P, 2 * NT, 6])
        ln_sum = sb("ln_sum", [P, 2 * NT, 2])
        ln_dif = sb("ln_dif", [P, 2 * NT])
        ln_sq = sb("ln_sq", [P, 2 * NT])
        ln_var = sb("ln_var", [P, 2 * NT])
        ln_mean = sb("ln_mean", [P, 2 * NT])
        ln_y = sb("ln_y", [P, 8, 2 * NT])
        ln_rstd = sb("ln_rstd", [P, 2 * NT])
        ln_off = sb("ln_off", [P, NT])
        q = sb("q", [P, NB, C])
        ll2 = sb("ll2", [P, NB, CH])
        ll_hl = sb("ll_hl", [P, NB, 2, CH], F32R)
        ll_t = sb("ll_t", [P, B, NPE], F32R)
        r = sb("r", [P, B, NT, C])

        g = [sb(f"g{u}", [P, KC, NPE]) for u in range(2)]
        g_hi = [sb(f"g_hi{u}", [P, KC, NPE], F32R) for u in range(2)]
        g_lo = [sb(f"g_lo{u}", [P, KC, NPE], F32R) for u in range(2)]
        u_sb = [sb(f"u_sb{u}", [P, NB * P]) for u in range(2)]
        o = [sb(f"o{u}", [P, NB, 2, C]) for u in range(2)]

        bank03 = ps("bank03", [P, 4, 512])
        bank45 = ps("bank45", [P, 2, 512])
        bank67 = ps("bank67", [P, 2, 512])
        wt_ps = bank03[:, 0:2, :].rearrange("p a (g c) -> p a g c", c=C)
        fc1t_ps, fold_ps = bank03[:, 2, :], bank03[:, 3, :]
        fc2t_ps = bank03[:, 0, 0:KC * CH]
        xa_ps, xb_ps = bank67[:, 0, 0:NPX], bank67[0:SPAN * PB, 1, 0:NP]
        y_ps = bank45
        s_ps = bank03.rearrange("p (u a) n -> p u a n", u=2)
        o_ps = bank45
        h_ps = bank67.rearrange("p a n -> p (a n)")[:, 0:NT * C].rearrange("p (t c) -> p t c", c=C)
        zt_ps = bank67.bitcast(FP16)
        ll_ps = bank67[:, 0, 0:NPE]
        f_ps = bank03
        u_ps = bank67
        d_ps = bank45
        ll_last_ps = bank45[:, 1, 0:NPE]

        cst_in = sem("cst_in")
        w_in = sem("w_in")
        col_in = sem("col_in")
        fc_in = sem("fc_in")
        x_in = [sem(f"x_in{u}") for u in range(2)]
        out_done = [sem(f"out_done{u}") for u in range(2)]
        cleared = sem("cleared")
        ident16_ok = sem("ident16_ok")
        wb_ok = sem("wb_ok")
        wt_tr = sem("wt_tr")
        w_hi_ok, w_lo_ok = sem("w_hi_ok"), sem("w_lo_ok")
        x_tr = sem("x_tr")
        x_hi_ok, x_lo_ok = sem("x_hi_ok"), sem("x_lo_ok")
        y_mm = sem("y_mm")
        y_ok = sem("y_ok")
        y_st = sem("y_st")
        bn_step = sem("bn_step")
        bn_ok = sem("bn_ok")
        fct_tr = sem("fct_tr")
        fct_ok = sem("fct_ok")
        table_ok = sem("table_ok")
        fold_mm = sem("fold_mm")
        fold_ok = sem("fold_ok")
        h_ch_ok = sem("h_ch_ok")
        h_tr = sem("h_tr")
        h_ok = sem("h_ok")
        st2_ok = sem("st2_ok")
        off_ok = sem("off_ok")
        ln_step = sem("ln_step")
        z_ok, z_hi_ok, z_lo_ok = sem("z_ok"), sem("z_hi_ok"), sem("z_lo_ok")
        z_tr = sem("z_tr")
        zt_hi_ok, zt_lo_ok = sem("zt_hi_ok"), sem("zt_lo_ok")
        s_mm = sem("s_mm")
        e_ok = sem("e_ok")
        o_mm = sem("o_mm")
        rden_ok, h2_ok, n_ok = sem("rden_ok"), sem("h2_ok"), sem("n_ok")
        q_ok, ll2_ok, ll_hi_ok, ll_lo_ok = sem("q_ok"), sem("ll2_ok"), sem("ll_hi_ok"), sem("ll_lo_ok")
        r_ok = sem("r_ok")
        ll_tr = sem("ll_tr")
        ll_t_ok = sem("ll_t_ok")
        f_mm = sem("f_mm")
        g_ok = sem("g_ok")
        g_hi_dve, g_hi_act = sem("g_hi_dve"), sem("g_hi_act")
        g_lo_dve, g_lo_pool = sem("g_lo_dve"), sem("g_lo_pool")
        u_mm, u_ok, d_mm, o_ok = sem("u_mm"), sem("u_ok"), sem("d_mm"), sem("o_ok")

        block = ctx.enter_context(nc.Block())

        x_v = x.rearrange("b (p two) d -> b p (two d)", two=2)
        out_v = out.rearrange("b (p two) c -> b p (two c)", two=2)
        FULL = P * (NB - 1)

        def tile_cols(i):
            return (i // NB) * NP + (i % NB) * P

        @block.sync
        def _(sp):
            def load_x(b, u):
                for s in range(SPAN):
                    lo, w, at = (0, PF, 0) if s == 0 else (P, PB, P + s * PB)
                    last = (XROWS if s == 0 else ROWS)[-1]
                    sp.dma_start(xin[u][:, 0:NB - 1, at:at + w],
                                 x_v[b, s:s + FULL, lo:lo + w].rearrange("(j p) n -> p j n", p=P))\
                      .then_inc(x_in[u], 16)
                    sp.dma_start(xin[u][0:last, NB - 1, at:at + w],
                                 x_v[b, s + FULL:s + FULL + last, lo:lo + w]).then_inc(x_in[u], 16)

            load_x(0, 0)
            load_x(1, 1)
            for col, src in ((bias_c, tok_b), (gamma_c, tok_gamma), (beta_c, tok_beta)):
                sp.dma_start(col[:, :], src.rearrange("(p a) -> p a", a=1)).then_inc(col_in, 16)
            for k in range(KC):
                sp.dma_start(fc1_bias[:, k:k + 1], fc1_b[P * k:P * k + P].rearrange("(p a) -> p a", a=1))\
                  .then_inc(col_in, 16)
            sp.dma_start(fc2_bias[0:CH, :], fc2_b.rearrange("(p a) -> p a", a=1)).then_inc(col_in, 16)
            sp.dma_start(fc1_rows[:, :, :], fc1_w.rearrange("(k p) c -> p k c", p=P)).then_inc(fc_in, 16)
            sp.dma_start(fc2_rows[:, :], fc2_w).then_inc(fc_in, 16)
            with sp.Fori(1, B // 2) as i:
                for u in range(2):
                    sp.wait_ge(x_tr, 2 * i + u - 1)
                    load_x(2 * i + u, u)

            def store(b, u, turn):
                sp.wait_ge(o_ok, b + 1)
                sp.dma_start(out_v[b, 0:FULL, :].rearrange("(j p) n -> p j n", p=P),
                             o[u][:, 0:NB - 1, :, :].rearrange("p j t c -> p j (t c)"))\
                  .then_inc(out_done[u], 16)
                sp.dma_start(out_v[b, FULL:NP, :],
                             o[u][0:ROWS[-1], NB - 1, :, :].rearrange("p t c -> p (t c)"))\
                  .then_inc(out_done[u], 16)

            with sp.Fori(0, B // 2) as i:
                for u in range(2):
                    store(2 * i + u, u, i)
            for u in range(2):
                sp.wait_ge(out_done[u], 32 * (B // 2))

        @block.gpsimd
        def _(pool):
            pool.memset(shift_c[:, :], SHIFT).then_inc(cleared, 1)
            pool.memset(wpad[:, 0:D], 0.0)
            pool.memset(wpad[:, D + TAPS * D:], 0.0).then_inc(cleared, 1)
            for u in range(2):
                pool.memset(xa_hi[u][:, NPX:NPX + 1].bitcast(FP32), 0.0)
                pool.memset(xa_lo[u][:, NPX:NPX + 1].bitcast(FP32), 0.0)
                pool.memset(xb_hi[u][:, NP:NPE].bitcast(FP32), 0.0)
                pool.memset(xb_lo[u][:, NP:NPE].bitcast(FP32), 0.0)
            pool.memset(y[:, B * T:], 0.0)
            pool.memset(zt_hi[:, 2 * NPE:], 0.0)
            pool.memset(zt_lo[:, 2 * NPE:], 0.0)
            pool.memset(e[:, :, T:], 1.0)
            pool.memset(u_sb[0][:, NPE:], 0.0)
            pool.memset(u_sb[1][:, NPE:], 0.0).then_inc(r_ok, 1)
            for u in range(2):
                pool.memset(z[u][:, :, C:C + 1], 1.0).then_inc(cleared, 1)

            def residual(b):
                pool.wait_ge(n_ok, b + 1)
                pool.tensor_tensor(r[:, b, :, :].rearrange("p t c -> p (t c)"),
                                   h2[:, :, :].rearrange("p t c -> p (t c)"),
                                   n[:, :, :].rearrange("p t c -> p (t c)"), ALU.add).then_inc(r_ok, 1)

            with pool.Fori(0, B - 1) as b:
                residual(b)

            def split_g(b, u):
                if not (isinstance(b, int) and b < 2):
                    pool.wait_ge(u_mm, b - 1)
                for k in range(KC - 1):
                    pool.wait_ge(g_hi_act, (KC - 1) * b + k + 1)
                    pool.tensor_tensor(g_lo[u][:, k, :], g[u][:, k, :],
                                       g_hi[u][:, k, :].bitcast(FP32), ALU.subtract).then_inc(g_lo_pool, 1)

            split_g(0, 0)
            split_g(1, 1)
            split_g(2, 0)
            residual(B - 1)
            split_g(3, 1)
            with pool.Fori(2, B // 2) as i:
                for u in range(2):
                    split_g(2 * i + u, u)

        @block.tensor
        def _(pe):
            pe.wait_ge(cst_in, 16)
            pe.wait_ge(w_in, 16)
            pe.wait_ge(cleared, 2)
            for par in range(2):
                off = D * (1 - par)
                for s in range(SPAN):
                    nc.tensor.transpose(wt_ps[:, par, s, :], wpad[:, off + PF * s:off + PF * s + P], ident)
            pe.wait_ge(wb_ok, 1)
            for par in range(2):
                last = nc.tensor.transpose(wt_ps[0:SPAN * PB, par, SPAN, :],
                                           wb[:, par, :, :].rearrange("p s n -> p (s n)"), ident)
            last.then_inc(wt_tr, 1)

            def transpose_x(b, u, turn):
                pe.wait_ge(x_in[u], 16 * X_DMAS * (turn + 1))
                if not (isinstance(b, int) and b == 0):
                    pe.wait_ge(x_lo_ok, b)
                for j in range(NB):
                    nc.tensor.transpose(xa_ps[:, P * j:P * j + XROWS[j]], xin[u][0:XROWS[j], j, 0:P],
                                        ident[0:XROWS[j], 0:XROWS[j]])
                for j in range(NB):
                    last = nc.tensor.transpose(xb_ps[:, P * j:P * j + ROWS[j]], xin[u][0:ROWS[j], j, P:XW],
                                               ident[0:ROWS[j], 0:ROWS[j]])
                last.then_inc(x_tr, 1)

            def context_products(b, u):
                for par in range(2):
                    if not (isinstance(b, int) and b == 0):
                        pe.wait_ge(y_ok, 2 * b - 1 + par)
                    k = 0
                    for w, (xa, xb), ready in ((w_hi, (xa_hi, xb_hi), x_hi_ok), (w_hi, (xa_lo, xb_lo), x_lo_ok),
                                               (w_lo, (xa_hi, xb_hi), None)):
                        if par == 0 and ready is not None:
                            pe.wait_ge(ready, b + 1)
                        if par == 0 and ready is None and isinstance(b, int) and b == 0:
                            pe.wait_ge(w_lo_ok, 1)
                        for s in range(SPAN + 1):
                            if s < SPAN:
                                lhs, rhs = w[:, par, s, :], xa[u][:, s:s + NPE]
                            else:
                                lhs, rhs = w[0:SPAN * PB, par, s, :], xb[u][:, :]
                            last = nc.tensor.matmul(y_ps[:, par, 0:NPE], lhs, rhs,
                                                    start=(k == 0), stop=(k == 3 * (SPAN + 1) - 1))
                            k += 1
                    last.then_inc(y_mm, 1)
                    if par == 0 and isinstance(b, int) and b == 0:
                        transpose_x(1, 1, 0)

            transpose_x(0, 0, 0)
            pe.wait_ge(w_hi_ok, 1)
            pe.wait_ge(cleared, 4)
            context_products(0, 0)
            with pe.Fori(0, B // 2 - 1) as i:
                transpose_x(2 * i + 2, 0, i + 1)
                context_products(2 * i + 1, 1)
                transpose_x(2 * i + 3, 1, i + 1)
                context_products(2 * i + 2, 0)
            context_products(B - 1, 1)

            pe.wait_ge(fc_in, 32)
            for k in range(KC):
                last = nc.tensor.transpose(fc1t_ps[:, P * k:P * k + P], fc1_rows[:, k, :], ident)
            last.then_inc(ll_tr, 1)
            for k in range(KC):
                last = nc.tensor.transpose(fc2t_ps[:, CH * k:CH * k + CH], fc2_rows[:, P * k:P * k + P],
                                           ident[0:CH, 0:CH])
            last.then_inc(fct_tr, 1)
            pe.wait_ge(fct_ok, 1)
            nc.tensor.matmul(fold_ps, interp2, fc1_t[:, :], start=True, stop=True).then_inc(fold_mm, 1)

            def transpose_h(b):
                pe.wait_ge(h_ch_ok, b + 1)
                if isinstance(b, int) and b == 0:
                    pe.wait_ge(x_lo_ok, B)
                else:
                    pe.wait_ge(zt_hi_ok, b)
                    pe.wait_ge(zt_lo_ok, b)
                    if not (isinstance(b, int) and b == 1):
                        pe.wait_ge(ll_t_ok, b - 1)
                for i in range(NT):
                    at = tile_cols(i)
                    last = nc.tensor.transpose(h_ps[:, i, :], h_ch[:, at:at + P], ident)
                last.then_inc(h_tr, 1)

            def transpose_z(b):
                pe.wait_ge(z_hi_ok, b + 1)
                for part, zs in enumerate((z_hi, z_lo)):
                    if part:
                        pe.wait_ge(z_lo_ok, b + 1)
                    for i in range(NT):
                        par, j = i // NB, i % NB
                        rows = min(P, NPE - P * j)
                        at = par * NPE + P * j
                        last = nc.tensor.transpose(zt_ps[:, part, at:at + rows], zs[0:rows, i, :],
                                                   ident16[0:rows, 0:rows])
                    last.then_inc(z_tr, 1)

            def transpose_ll(b, dst):
                pe.wait_ge(ll_lo_ok, b + 1)
                for j in range(NB):
                    rows = min(P, NPE - P * j)
                    last = nc.tensor.transpose(dst[:, P * j:P * j + rows],
                                               ll_hl[0:rows, j, :, :].rearrange("p a c -> p (a c)").bitcast(FP32),
                                               ident[0:rows, 0:rows])
                last.then_inc(ll_tr, 1)

            def scores(b, i):
                at = (i // NB) * NPE + (i % NB) * P
                if not (isinstance(b, int) and b == 0 and i < 2):
                    pe.wait_ge(e_ok, NT * b + i - 1)
                for par in range(2):
                    cols = slice(par * NPE, par * NPE + NP)
                    dst = s_ps[:, i % 2, par, 0:NP]
                    nc.tensor.matmul(dst, zt_hi[:, at:at + P], zt_hi[:, cols], start=True, stop=False)
                    nc.tensor.matmul(dst, zt_hi[:, at:at + P], zt_lo[:, cols], start=False, stop=False)
                    last = nc.tensor.matmul(dst, zt_lo[:, at:at + P], zt_hi[:, cols], start=False, stop=True)
                last.then_inc(s_mm, 1)

            def attend(b, zu, i):
                par, j = i // NB, i % NB
                if j == 0:
                    if isinstance(b, int) and b == 0:
                        pe.wait_ge(y_ok, 2 * B)
                    else:
                        pe.wait_ge(h2_ok, 2 * b - 1 + par)
                for k in range(NT):
                    if i == 0:
                        pe.wait_ge(e_ok, NT * b + k + 1)
                    rows = ROWS[k % NB]
                    last = nc.tensor.matmul(o_ps[:, par, j * (C + 1):(j + 1) * (C + 1)],
                                            e[0:rows, k, tile_cols(i):tile_cols(i) + P],
                                            z[zu][0:rows, k, :], start=(k == 0), stop=(k == NT - 1))
                if j == NB - 1:
                    last.then_inc(o_mm, 1)

            def hidden(b):
                pe.wait_ge(ll_t_ok, b + 2)
                for k in range(KC):
                    if isinstance(b, int) and b == 0:
                        pe.wait_ge(e_ok, B * NT)
                    else:
                        pe.wait_ge(g_ok, KC * b - (KC - 1) + k)
                    rhs = ll_t[:, b, :]
                    nc.tensor.matmul(f_ps[:, k, 0:NPE], fc1_hi[:, P * k:P * k + P], rhs, start=True, stop=False)
                    nc.tensor.matmul(f_ps[:, k, 0:NPE], fc1_lo[:, P * k:P * k + P], rhs, start=False, stop=True)\
                      .then_inc(f_mm, 1)

            def attention(b, u, first=False, last=False):
                pe.wait_ge(zt_hi_ok, b + 1)
                pe.wait_ge(zt_lo_ok, b + 1)
                scores(b, 0)
                scores(b, 1)
                if not last:
                    transpose_h(b + 1)
                for i in range(2, NT):
                    scores(b, i)
                attend(b, u, 0)
                attend(b, u, 1)
                if last:
                    hidden(0)
                attend(b, u, 2)
                attend(b, u, 3)
                if last:
                    hidden(1)
                else:
                    pe.wait_ge(h_ok, b + 2)
                    transpose_z(b + 1)
                attend(b, u, 4)
                if not first:
                    if not last:
                        pe.wait_ge(zt_hi_ok, b + 2)
                    transpose_ll(b - 1, ll_ps)
                attend(b, u, 5)

            pe.wait_ge(ident16_ok, 1)
            transpose_h(0)
            pe.wait_ge(h_ok, 1)
            transpose_z(0)
            pe.wait_ge(fold_ok, 1)
            attention(0, 0, first=True)
            with pe.Fori(0, B // 2 - 1) as i:
                attention(2 * i + 1, 1)
                attention(2 * i + 2, 0)
            attention(B - 1, 1, last=True)

            def project(b, u):
                if isinstance(b, int) and b < 2:
                    pe.wait_ge(ll_t_ok, B)
                else:
                    pe.wait_ge(u_ok, b - 1)
                for k in range(KC):
                    if k == KC - 1:
                        pe.wait_ge(g_hi_dve, b + 1)
                    else:
                        pe.wait_ge(g_hi_act, (KC - 1) * b + k + 1)
                    lhs = fc2_hl[:, k, :, :].rearrange("p a c -> p (a c)")
                    nc.tensor.matmul(u_ps[:, u, 0:NPE], lhs, g_hi[u][:, k, :], start=(k == 0), stop=False)
                    if k == KC - 1:
                        pe.wait_ge(g_lo_dve, b + 1)
                    else:
                        pe.wait_ge(g_lo_pool, (KC - 1) * b + k + 1)
                    last = nc.tensor.matmul(u_ps[:, u, 0:NPE], lhs, g_lo[u][:, k, :], start=False, stop=(k == KC - 1))
                last.then_inc(u_mm, 1)

            def spread(b, u):
                pe.wait_ge(u_ok, b + 1)
                if isinstance(b, int) and b == 0:
                    pe.wait_ge(h2_ok, 2 * B)
                elif isinstance(b, int) and b == 1:
                    pe.wait_ge(ll_t_ok, B + 1)
                else:
                    pe.wait_ge(o_ok, b - 1)
                for j in range(NB):
                    last = nc.tensor.matmul(d_ps[:, u, C * j:C * j + C], u_sb[u][:, P * j:P * j + P], dup,
                                            start=True, stop=True)
                last.then_inc(d_mm, 1)

            project(0, 0)
            hidden(2)
            project(1, 1)
            spread(0, 0)
            hidden(3)
            project(2, 0)
            pe.wait_ge(h2_ok, 2 * B)
            transpose_ll(B - 1, ll_last_ps)
            spread(1, 1)
            with pe.Fori(2, B // 2) as i:
                for u in range(2):
                    hidden(2 * i + u)
                    project(2 * i + u - 1, 1 - u)
                    spread(2 * i + u - 2, u)
            project(B - 1, 1)
            spread(B - 2, 0)
            spread(B - 1, 1)

        @block.scalar
        def _(act):
            act.dma_start(wpad[:, D:D + TAPS * D], tok_w).then_inc(w_in, 16)
            act.dma_start(cst[:, :], consts).then_inc(cst_in, 16)
            act.wait_ge(cleared, 1)
            nc.scalar.activation(bn_off[:, :], shift_c[:, :], ACT.Exp).then_inc(table_ok, 1)
            act.wait_ge(wt_tr, 1)
            nc.scalar.activation(w_hi[:, :, 0:SPAN, :], wt_ps[:, :, 0:SPAN, :], ACT.Copy)\
              .then_inc(ll_t_ok, 1)
            nc.scalar.activation(w_hi[0:SPAN * PB, :, SPAN, :], wt_ps[0:SPAN * PB, :, SPAN, :], ACT.Copy)\
              .then_inc(w_hi_ok, 1)

            def frames_hi(b, u):
                act.wait_ge(x_tr, b + 1)
                if not (isinstance(b, int) and b < 2):
                    act.wait_ge(y_mm, 2 * b - 2)
                nc.scalar.activation(xa_hi[u][:, 0:NPX], xa_ps, ACT.Copy)
                nc.scalar.activation(xb_hi[u][:, 0:NP], xb_ps, ACT.Copy).then_inc(x_hi_ok, 1)

            def relu(b):
                for par in range(2):
                    act.wait_ge(y_mm, 2 * b + par + 1)
                    nc.scalar.activation(y[:, bass.ds(b * T + par * NP, NP)], y_ps[:, par, 0:NP], ACT.Relu,
                                         bias=bias_c[:, :]).then_inc(y_ok, 1)

            frames_hi(0, 0)
            act.wait_ge(col_in, 16 * (4 + KC))
            frames_hi(1, 1)
            relu(0)
            with act.Fori(0, B // 2 - 1) as i:
                frames_hi(2 * i + 2, 0)
                relu(2 * i + 1)
                frames_hi(2 * i + 3, 1)
                relu(2 * i + 2)
            relu(B - 1)

            nc.scalar.activation(ident16[:, :], ident, ACT.Copy).then_inc(ident16_ok, 1)
            act.wait_ge(fct_tr, 1)
            nc.scalar.activation(fc1_t[:, :], fc1t_ps, ACT.Copy).then_inc(fct_ok, 1)
            nc.scalar.activation(fc2_hl[:, :, 0, :], fc2t_ps.rearrange("p (k c) -> p k c", c=CH), ACT.Copy)\
              .then_inc(fct_ok, 1)
            act.wait_ge(fold_mm, 1)
            nc.scalar.activation(fc1_hi[:, :], fold_ps, ACT.Copy).then_inc(fct_ok, 1)

            def normalise_channels(b):
                if isinstance(b, int) and b == 0:
                    act.wait_ge(bn_ok, 2)
                else:
                    act.wait_ge(h_tr, b)
                nc.scalar.activation(h_ch[:, :], y[:, bass.ds(b * T, TPAD)], ACT.Identity,
                                     bias=bn_shift[:, :], scale=bn_scale[:, :]).then_inc(h_ch_ok, 1)

            def copy_h(b, u):
                act.wait_ge(h_tr, b + 1)
                if not (isinstance(b, int) and b < 2):
                    act.wait_ge(h2_ok, 2 * b - 2)
                nc.scalar.activation(h[u][:, :, :], h_ps, ACT.Copy).then_inc(h_ok, 1)

            def exponentials(b, i):
                act.wait_ge(s_mm, NT * b + i + 1)
                if i == 0 and not (isinstance(b, int) and b == 0):
                    act.wait_ge(o_mm, 2 * b)
                nc.scalar.activation(e[:, i, 0:T].rearrange("p (a n) -> p a n", a=2), s_ps[:, i % 2, :, 0:NP],
                                     ACT.Exp, bias=shift_c[:, :]).then_inc(e_ok, 1)

            def copy_zt_hi(b):
                act.wait_ge(z_tr, 2 * b + 1)
                if not (isinstance(b, int) and b == 0):
                    act.wait_ge(s_mm, NT * b)
                nc.scalar.activation(zt_hi[:, 0:2 * NPE], zt_ps[:, 0, 0:2 * NPE], ACT.Copy).then_inc(zt_hi_ok, 1)

            def second_norm(b):
                act.wait_ge(off_ok, b + 1)
                act.wait_ge(r_ok, b + 1)
                for i in range(NT):
                    last = nc.scalar.activation(n[:, i, :], h2[:, i, :], ACT.Identity,
                                                bias=ln_off[:, i:i + 1], scale=ln_rstd[:, i:i + 1])
                last.then_inc(n_ok, 1)

            def copy_ll(b, src):
                act.wait_ge(ll_tr, b + 2)
                nc.scalar.activation(ll_t[:, b, :], src, ACT.Copy).then_inc(ll_t_ok, 1)

            def attention(b, u, first=False, last=False):
                exponentials(b, 0)
                exponentials(b, 1)
                if not last:
                    copy_h(b + 1, 1 - u)
                for i in range(2, NT):
                    exponentials(b, i)
                if not last and not (isinstance(b, int) and b == B - 2):
                    normalise_channels(b + 2)
                if not first:
                    second_norm(b - 1)
                if not last:
                    copy_zt_hi(b + 1)
                if last:
                    gelu(0, 0)
                    gelu(1, 1)
                if not first:
                    copy_ll(b - 1, ll_ps)

            def gelu(b, u):
                for k in range(KC):
                    act.wait_ge(f_mm, KC * b + k + 1)
                    if k == 0 and not (isinstance(b, int) and b < 2):
                        act.wait_ge(g_lo_dve, b - 1)
                        act.wait_ge(g_lo_pool, (KC - 1) * (b - 1))
                    nc.scalar.activation(g[u][:, k, :], f_ps[:, k, 0:NPE], ACT.Gelu,
                                         bias=fc1_bias[:, k:k + 1]).then_inc(g_ok, 1)
                    if k == 1 and not (isinstance(b, int) and b < 2):
                        act.wait_ge(u_mm, b - 1)
                    if k > 0:
                        act.wait_ge(g_ok, KC * b + k)
                        nc.scalar.activation(g_hi[u][:, k - 1, :], g[u][:, k - 1, :], ACT.Copy)\
                          .then_inc(g_hi_act, 1)

            normalise_channels(0)
            copy_h(0, 0)
            normalise_channels(1)
            copy_zt_hi(0)
            attention(0, 0, first=True)
            with act.Fori(0, B // 2 - 2) as i:
                attention(2 * i + 1, 1)
                attention(2 * i + 2, 0)
            attention(B - 3, 1)
            attention(B - 2, 0)
            attention(B - 1, 1, last=True)
            gelu(2, 0)
            second_norm(B - 1)
            gelu(3, 1)
            copy_ll(B - 1, ll_last_ps)
            with act.Fori(2, B // 2) as i:
                for u in range(2):
                    gelu(2 * i + u, u)

        @block.vector
        def _(dve):
            nc.vector.memset(fc2_bias[CH:, :], 0.0)
            dve.wait_ge(w_in, 16)
            dve.wait_ge(cleared, 2)
            for par in range(2):
                at = D * (1 - par) + P
                last = nc.vector.tensor_copy(
                    wb[:, par, :, :], wpad[:, at:at + SPAN * PF].rearrange("p (s n) -> p s n", n=PF)[:, :, 0:PB])
            last.then_inc(wb_ok, 1)
            def frames_lo(b, u):
                dve.wait_ge(x_hi_ok, b + 1)
                nc.vector.tensor_tensor(xa_lo[u][:, 0:NPX], xa_ps, xa_hi[u][:, 0:NPX].bitcast(FP32), ALU.subtract)
                nc.vector.tensor_tensor(xb_lo[u][:, 0:NP], xb_ps, xb_hi[u][:, 0:NP].bitcast(FP32), ALU.subtract)\
                  .then_inc(x_lo_ok, 1)

            def channel_stats(b):
                for par in range(2):
                    dve.wait_ge(y_ok, 2 * b + par + 1)
                    nc.vector.bn_stats(bn[:, bass.ds(2 * b + par, 1), :].rearrange("p a s -> p (a s)"),
                                       y[:, bass.ds(b * T + par * NP, NP)]).then_inc(y_st, 1)

            frames_lo(0, 0)
            dve.wait_ge(w_hi_ok, 1)
            nc.vector.tensor_tensor(w_lo[:, :, 0:SPAN, :], wt_ps[:, :, 0:SPAN, :],
                                    w_hi[:, :, 0:SPAN, :].bitcast(FP32), ALU.subtract)
            nc.vector.tensor_tensor(w_lo[0:SPAN * PB, :, SPAN, :], wt_ps[0:SPAN * PB, :, SPAN, :],
                                    w_hi[0:SPAN * PB, :, SPAN, :].bitcast(FP32), ALU.subtract)\
              .then_inc(w_lo_ok, 1)

            frames_lo(1, 1)
            channel_stats(0)
            with dve.Fori(0, B // 2 - 1) as i:
                frames_lo(2 * i + 2, 0)
                channel_stats(2 * i + 1)
                frames_lo(2 * i + 3, 1)
                channel_stats(2 * i + 2)
            channel_stats(B - 1)

            def rsqrt(out, v, y, scale, done, at):
                def link(instruction):
                    nonlocal at
                    at = at + 1
                    instruction.then_inc(done, 1)
                    dve.wait_ge(done, at)

                I32 = mybir.dt.int32
                link(nc.vector.tensor_scalar(y[0].bitcast(I32), v.bitcast(I32), 1, None, ALU.logical_shift_right))
                link(nc.vector.tensor_scalar(y[1].bitcast(I32), y[0].bitcast(I32), -1.0, float(0x5F3759DF),
                                             ALU.mult, ALU.add))
                for k, s in ((1, 1.0), (3, 1.0), (5, scale)):
                    dst = out if k == 5 else y[k + 2]
                    link(nc.vector.tensor_tensor(y[0], y[k], y[k], ALU.mult))
                    link(nc.vector.scalar_tensor_tensor(y[k + 1], y[0], -0.5 * s, v, ALU.mult, ALU.mult))
                    link(nc.vector.scalar_tensor_tensor(dst, y[k + 1], 1.5 * s, y[k], ALU.add, ALU.mult))

            dve.wait_ge(y_st, 2 * B)
            nc.vector.bn_aggr(bn_mv[:, :], bn[:, :, :].rearrange("p a s -> p (a s)")).then_inc(bn_step, 1)
            dve.wait_ge(bn_step, 1)
            nc.vector.tensor_scalar_add(bn_var[:, :], bn_mv[:, 1:2], EPS).then_inc(bn_step, 1)
            dve.wait_ge(bn_step, 2)
            rsqrt(bn_y[:, 7:8], bn_var[:, :], [bn_y[:, k:k + 1] for k in range(7)], 1.0, bn_step, 2)
            nc.vector.tensor_tensor(bn_scale[:, :], bn_y[:, 7:8], gamma_c[:, :], ALU.mult).then_inc(bn_ok, 1)
            dve.wait_ge(bn_ok, 1)
            dve.wait_ge(table_ok, 1)
            nc.vector.tensor_tensor(bn_off[:, :], bn_mv[:, 0:1], bn_scale[:, :], ALU.mult)\
              .then_inc(bn_step, 1)
            dve.wait_ge(bn_step, 2 + RSQRT_STEPS + 1)
            nc.vector.tensor_tensor(bn_shift[:, :], beta_c[:, :], bn_off[:, :], ALU.subtract)\
              .then_inc(bn_ok, 1)

            def feed_forward_lows():
                dve.wait_ge(fct_ok, 3)
                nc.vector.tensor_tensor(fc2_hl[:, :, 1, :], fc2t_ps.rearrange("p (k c) -> p k c", c=CH),
                                        fc2_hl[:, :, 0, :].bitcast(FP32), ALU.subtract)
                nc.vector.tensor_tensor(fc1_lo[:, :], fold_ps, fc1_hi[:, :].bitcast(FP32), ALU.subtract)\
                  .then_inc(fold_ok, 1)

            def add_attention(b, u):
                for par in range(2):
                    dve.wait_ge(o_mm, 2 * b + par + 1)
                    ov = o_ps[:, par, 0:NB * (C + 1)].rearrange("p (j c) -> p j c", c=C + 1)
                    nc.vector.reciprocal(rden[:, NB * par:NB * par + NB], ov[:, :, C]).then_inc(rden_ok, 1)
                    dve.wait_ge(rden_ok, 2 * b + par + 1)
                    if par == 0:
                        dve.wait_ge(r_ok, b + 1)
                    for j in range(NB):
                        i = NB * par + j
                        last = nc.vector.scalar_tensor_tensor(h2[:, i, :], ov[:, j, 0:C], rden[:, i:i + 1],
                                                              h[u][:, i, :], ALU.mult, ALU.add)
                    last.then_inc(h2_ok, 1)
                dve.wait_ge(h2_ok, 2 * b + 2)
                for i in range(NT):
                    last = nc.vector.bn_stats(ln[:, i, :], h2[:, i, :])
                last.then_inc(st2_ok, 1)

            def first_stats(b, u):
                dve.wait_ge(h_ok, b + 1)
                for i in range(NT):
                    last = nc.vector.bn_stats(ln[:, NT + i, :], h[u][:, i, :])
                last.then_inc(st2_ok, 1)

            def layer_norms(lo, hi, turn, stats):
                at = LN_STEPS * turn
                dve.wait_ge(st2_ok, stats)
                nc.vector.tensor_tensor(ln_dif[:, lo:hi], ln[:, lo:hi, 1], ln[:, lo:hi, 4], ALU.subtract)\
                  .then_inc(ln_step, 1)
                nc.vector.tensor_tensor(ln_sum[:, lo:hi, :], ln[:, lo:hi, 1:3], ln[:, lo:hi, 4:6], ALU.add)\
                  .then_inc(ln_step, 1)
                dve.wait_ge(ln_step, at + 1)
                nc.vector.scalar_tensor_tensor(ln_sq[:, lo:hi], ln_dif[:, lo:hi], C / 4.0, ln_dif[:, lo:hi],
                                               ALU.mult, ALU.mult).then_inc(ln_step, 1)
                dve.wait_ge(ln_step, at + 3)
                nc.vector.scalar_tensor_tensor(ln_var[:, lo:hi], ln_sq[:, lo:hi], C * EPS, ln_sum[:, lo:hi, 1],
                                               ALU.add, ALU.add).then_inc(ln_step, 1)
                nc.vector.tensor_scalar(ln_mean[:, lo:hi], ln_sum[:, lo:hi, 0], 0.5, None, ALU.mult)\
                  .then_inc(ln_step, 1)
                dve.wait_ge(ln_step, at + 5)
                rsqrt(ln_rstd[:, lo:hi], ln_var[:, lo:hi], [ln_y[:, k, lo:hi] for k in range(7)],
                      float(C) ** 0.5, ln_step, at + 5)

            def second_offsets():
                nc.vector.scalar_tensor_tensor(ln_off[:, :], ln_mean[:, 0:NT], -1.0, ln_rstd[:, 0:NT],
                                               ALU.mult, ALU.mult).then_inc(off_ok, 1)

            def band(b):
                dve.wait_ge(n_ok, b + 1)
                nc.vector.tensor_tensor(q[:, :, :], n[:, 0:NB, :], n[:, NB:NT, :], ALU.add).then_inc(q_ok, 1)
                dve.wait_ge(q_ok, b + 1)
                qv = q[:, :, :].rearrange("p j (c two) -> p j c two", two=2)
                nc.vector.tensor_tensor(ll2[:, :, :], qv[:, :, :, 0], qv[:, :, :, 1], ALU.add).then_inc(ll2_ok, 1)
                dve.wait_ge(ll2_ok, b + 1)
                dve.wait_ge(ll_tr, b + 1)
                nc.vector.tensor_scalar(ll_hl[:, :, 0, :], ll2[:, :, :], 0.5, None, ALU.mult).then_inc(ll_hi_ok, 1)
                dve.wait_ge(ll_hi_ok, b + 1)
                nc.vector.scalar_tensor_tensor(ll_hl[:, :, 1, :], ll2[:, :, :], 0.5,
                                               ll_hl[:, :, 0, :].bitcast(FP32), ALU.mult, ALU.subtract)\
                  .then_inc(ll_lo_ok, 1)

            def first_norm(b, u):
                if not (isinstance(b, int) and b < 2):
                    dve.wait_ge(o_mm, 2 * b - 2)
                for i in range(NT):
                    last = nc.vector.tensor_scalar(z[u][:, i, 0:C], h[u][:, i, :], ln_mean[:, NT + i:NT + i + 1],
                                                   ln_rstd[:, NT + i:NT + i + 1], ALU.subtract, ALU.mult)
                last.then_inc(z_ok, 1)
                dve.wait_ge(z_ok, b + 1)
                if not (isinstance(b, int) and b == 0):
                    dve.wait_ge(z_tr, 2 * b)
                nc.vector.tensor_copy(z_hi[:, :, :], z[u][:, :, 0:C]).then_inc(z_hi_ok, 1)
                dve.wait_ge(z_hi_ok, b + 1)
                nc.vector.tensor_tensor(z_lo[:, :, :], z[u][:, :, 0:C], z_hi[:, :, :], ALU.subtract)\
                  .then_inc(z_lo_ok, 1)

            def copy_zt_lo(b):
                if not (isinstance(b, int) and b == 0):
                    dve.wait_ge(s_mm, NT * b)
                dve.wait_ge(z_tr, 2 * b + 2)
                nc.vector.tensor_copy(zt_lo[:, 0:2 * NPE], zt_ps[:, 1, 0:2 * NPE]).then_inc(zt_lo_ok, 1)

            def attention(b, u, first=False, last=False):
                if not first:
                    add_attention(b - 1, 1 - u)
                if not last:
                    first_stats(b + 1, 1 - u)
                layer_norms(NT if first else 0, NT if last else 2 * NT, b + 1, 2 * b + 2 if not last else 2 * B - 1)
                if not first:
                    second_offsets()
                if not last:
                    first_norm(b + 1, 1 - u)
                if not first:
                    band(b - 1)
                if not last:
                    copy_zt_lo(b + 1)

            feed_forward_lows()
            first_stats(0, 0)
            layer_norms(NT, 2 * NT, 0, 1)
            first_norm(0, 0)
            copy_zt_lo(0)
            attention(0, 0, first=True)
            with dve.Fori(0, B // 2 - 1) as i:
                attention(2 * i + 1, 1)
                attention(2 * i + 2, 0)
            attention(B - 1, 1, last=True)

            def split_g(b, u):
                if not (isinstance(b, int) and b < 2):
                    dve.wait_ge(u_mm, b - 1)
                dve.wait_ge(g_ok, KC * b + KC)
                k = KC - 1
                nc.vector.tensor_copy(g_hi[u][:, k, :], g[u][:, k, :]).then_inc(g_hi_dve, 1)
                dve.wait_ge(g_hi_dve, b + 1)
                nc.vector.tensor_tensor(g_lo[u][:, k, :], g[u][:, k, :], g_hi[u][:, k, :].bitcast(FP32),
                                        ALU.subtract).then_inc(g_lo_dve, 1)

            def band_change(b, u):
                dve.wait_ge(u_mm, b + 1)
                if not (isinstance(b, int) and b < 2):
                    dve.wait_ge(d_mm, b - 1)
                dve.wait_ge(ll_t_ok, b + 2)
                nc.vector.scalar_tensor_tensor(u_sb[u][:, 0:NPE], u_ps[:, u, 0:NPE], fc2_bias[:, :],
                                               ll_t[:, b, :].bitcast(FP32), ALU.add, ALU.subtract)\
                  .then_inc(u_ok, 1)

            def finish(b, u, turn):
                dve.wait_ge(d_mm, b + 1)
                dve.wait_ge(r_ok, b + 2)
                if not (isinstance(b, int) and b < 2):
                    dve.wait_ge(out_done[u], 32 * turn)
                dv = d_ps[:, u, 0:NB * C].rearrange("p (j c) -> p j c", c=C)
                rv = r[:, b, :, :]
                for par in range(2):
                    last = nc.vector.tensor_tensor(o[u][:, :, par, :], dv, rv[:, NB * par:NB * par + NB, :],
                                                   ALU.add)
                last.then_inc(o_ok, 1)

            split_g(0, 0)
            split_g(1, 1)
            add_attention(B - 1, 1)
            layer_norms(0, NT, B + 1, 2 * B)
            second_offsets()
            band_change(0, 0)
            split_g(2, 0)
            band_change(1, 1)
            band(B - 1)
            split_g(3, 1)
            finish(0, 0, 0)
            band_change(2, 0)
            finish(1, 1, 0)
            with dve.Fori(2, B // 2) as i:
                split_g(2 * i, 0)
                band_change(2 * i - 1, 1)
                finish(2 * i - 2, 0, i - 1)
                split_g(2 * i + 1, 1)
                band_change(2 * i, 0)
                finish(2 * i - 1, 1, i - 1)
            band_change(B - 1, 1)
            finish(B - 2, 0, B // 2 - 1)
            finish(B - 1, 1, B // 2 - 1)


_INS = ['x', 'L0_tok_W', 'L0_tok_b', 'L0_tok_gamma', 'L0_tok_beta', 'L0_ffn_fc1_w', 'L0_ffn_fc1_b',
        'L0_ffn_fc2_w', 'L0_ffn_fc2_b']


def _shape_constants():
    import numpy as np
    pos = np.linspace(0.0, 1.0, C, dtype=np.float32) * np.float32(CH - 1)
    i0 = np.clip(np.floor(pos).astype(np.int32), 0, CH - 2)
    w = pos - i0.astype(np.float32)
    a = np.zeros((C, CH), np.float32)
    a[np.arange(C), i0] += np.float32(1.0) - w
    a[np.arange(C), i0 + 1] += w
    half = np.zeros((CH, C), np.float32)
    half[np.arange(C) // 2, np.arange(C)] = 0.5
    return np.concatenate([a, a, np.concatenate([half, half], 0), np.eye(P, dtype=np.float32)], 1)


def kernel(**inputs):
    import numpy as _np
    import concourse.bacc as _bacc
    from concourse import mybir as _mybir
    from concourse.bass_utils import run_bass_kernel_spmd as _run

    nc = _bacc.Bacc("TRN2", target_bir_lowering=False, num_devices=1)
    arrays, args = {}, []
    for name in _INS:
        arrays[f"in_{name}"] = _np.ascontiguousarray(inputs[name])
    arrays["in_consts"] = _shape_constants()
    for name, a in arrays.items():
        args.append(nc.dram_tensor(name, a.shape, _mybir.dt.from_np(a.dtype), kind="ExternalInput").ap())
    args.append(nc.dram_tensor("out", (B, T, C), _mybir.dt.float32, kind="ExternalOutput").ap())
    tower_kernel(nc, *args)
    r = _run(nc, [arrays], core_ids=[0])
    return r.results[0]["out"]
```

```python
import concourse.bass as bass
from concourse import mybir
from contextlib import ExitStack

FP32 = mybir.dt.float32
F32R = mybir.dt.float32r
FP16 = mybir.dt.float16
ALU = mybir.AluOpType
ACT = mybir.ActivationFunctionType

B, L, D = 8, 750, 80
TAPS = 5
C = 128
HID = 512
T = L - (TAPS - 1)
NP = T // 2
P = 128
EPS = 1e-5

NB = -(-NP // P)
NT = 2 * NB
ROWS = [min(P, NP - P * j) for j in range(NB)]
NPE = NP + 1
TPAD = NP + P * NB
ZW = 2 * NPE + P

PF = 2 * D
PB = PF - P
SPAN = 3
NPX = L // 2
XROWS = [min(P, NPX - P * j) for j in range(NB)]
XW = P + SPAN * PB
WPAD = D + P + SPAN * PF
X_DMAS = 5

KC = HID // P
CH = C // 2
RSQRT_STEPS = 10
LN_STEPS = 5 + RSQRT_STEPS
WARM_START = 9
WARM_NORM, WARM_Z = 6, 20
HIGH_ON_DVE = ((2, 3), (2, 3), (), (3,), (3,), (3,), (3,), (2, 3))
LOW_ON_DVE = ((3,), (3,), (), (3,), (3,), (3,), (3,), (3,))
SHIFT = -64.0


def tower_kernel(nc, x, tok_w, tok_b, tok_gamma, tok_beta, fc1_w, fc1_b, fc2_w, fc2_b, consts, out):
    ctx = ExitStack()
    with ctx:
        def sb(name, shape, dt=FP32):
            return ctx.enter_context(nc.sbuf_tensor(name, shape, dt))

        def ps(name, shape, dt=FP32):
            return ctx.enter_context(nc.psum_tensor(name, shape, dt))

        def sem(name):
            return ctx.enter_context(nc.semaphore(name))

        warm = sb("warm", [P, 512], FP16)
        cst = sb("cst", [P, 2 * P])
        interp2, dup = cst[:, 0:P], cst[:, P:2 * P]
        ident = sb("ident", [P, P])[:, :]
        ident16 = sb("ident16", [P, P], FP16)
        wpad = sb("wpad", [P, WPAD])
        wb = sb("wb", [P, 2, SPAN, PB])
        bias_c = sb("bias_c", [P, 1])
        gamma_c = sb("gamma_c", [P, 1])
        beta_c = sb("beta_c", [P, 1])
        fc1_rows = sb("fc1_rows", [P, KC, C])
        fc1_bias = sb("fc1_bias", [P, KC])
        fc2_rows = sb("fc2_rows", [CH, HID])
        fc2_bias = sb("fc2_bias", [P, 1])
        shift_c = sb("shift_c", [P, 1])
        w_hi = sb("w_hi", [P, 2, SPAN + 1, C], F32R)
        w_lo = sb("w_lo", [P, 2, SPAN + 1, C], F32R)
        fc1_t = sb("fc1_t", [C, HID])
        fc1_hi = sb("fc1_hi", [P, HID], F32R)
        fc1_lo = sb("fc1_lo", [P, HID], F32R)
        fc2_hl = sb("fc2_hl", [P, KC, 2, CH], F32R)

        xin = [sb(f"xin{u}", [P, NB, XW]) for u in range(2)]
        xa_hi = [sb(f"xa_hi{u}", [P, NPX + 1], F32R) for u in range(2)]
        xa_lo = [sb(f"xa_lo{u}", [P, NPX + 1], F32R) for u in range(2)]
        xb_hi = [sb(f"xb_hi{u}", [SPAN * PB, NPE], F32R) for u in range(2)]
        xb_lo = [sb(f"xb_lo{u}", [SPAN * PB, NPE], F32R) for u in range(2)]
        y = sb("y", [C, (B - 1) * T + TPAD])
        bn = sb("bn", [C, 2 * B, 6])
        bn_mv = sb("bn_mv", [C, 2])
        bn_var = sb("bn_var", [C, 1])
        bn_rstd = sb("bn_rstd", [C, 1])
        minus_half = sb("minus_half", [P, NT])
        table_c = sb("table_c", [C, 1])
        bn_mean_neg = sb("bn_mean_neg", [C, 1])
        bn_scale = sb("bn_scale", [C, 1])
        bn_shift = sb("bn_shift", [C, 1])

        h_ch = sb("h_ch", [C, TPAD])
        h = [sb(f"h{u}", [P, NT, C]) for u in range(2)]
        z = [sb(f"z{u}", [P, NT, C + 1]) for u in range(2)]
        z_hi = sb("z_hi", [P, NT, C], FP16)
        z_lo = sb("z_lo", [P, NT, C], FP16)
        zt_hi = sb("zt_hi", [C, ZW], FP16)
        zt_lo = sb("zt_lo", [C, ZW], FP16)
        e = sb("e", [P, NT, TPAD])
        rden = sb("rden", [P, NT])
        h2 = sb("h2", [P, NT, C])
        n = sb("n", [P, NT, C])
        ln = sb("ln", [P, 2 * NT, 6])
        ln_sum = sb("ln_sum", [P, 2 * NT, 2])
        ln_dif = sb("ln_dif", [P, 2 * NT])
        ln_sq = sb("ln_sq", [P, 2 * NT])
        ln_var = sb("ln_var", [P, 2 * NT])
        ln_mean = sb("ln_mean", [P, 2 * NT])
        ln_y = sb("ln_y", [P, 8, 2 * NT])
        ln_rstd = sb("ln_rstd", [P, 2 * NT])
        ln_off = sb("ln_off", [P, NT])
        q = sb("q", [P, NB, C])
        ll2 = sb("ll2", [P, NB, CH])
        ll_hl = sb("ll_hl", [P, NB, 2, CH], F32R)
        ll_t = sb("ll_t", [P, B, NPE], F32R)
        r = sb("r", [P, B, NB, 2, C])

        g = [sb(f"g{u}", [P, KC, NPE]) for u in range(2)]
        g_hi = [sb(f"g_hi{u}", [P, KC, NPE], F32R) for u in range(2)]
        g_lo = [sb(f"g_lo{u}", [P, KC, NPE], F32R) for u in range(2)]
        u_sb = [sb(f"u_sb{u}", [P, NB * P]) for u in range(2)]
        fc2_raw = g[0][:, 0, 0:KC * CH]
        fc1_raw = g[0][:, 1:3, :].rearrange("p k n -> p (k n)")[:, 0:HID]

        bank03 = ps("bank03", [P, 4, 512])
        bank45 = ps("bank45", [P, 2, 512])
        bank67 = ps("bank67", [P, 2, 512])
        wt_ps = bank03[:, 0:2, :].rearrange("p a (g c) -> p a g c", c=C)
        fc1t_ps, fold_ps = bank03[:, 2, :], bank03[:, 3, :]
        fc2t_ps = bank03[:, 0, 0:KC * CH]
        xa_ps, xb_ps = bank67[:, 0, 0:NPX], bank67[0:SPAN * PB, 1, 0:NP]
        y_ps = bank45
        s_ps = bank03.rearrange("p (u a) n -> p u a n", u=2)
        o_ps = bank45
        h_ps = bank67.rearrange("p a n -> p (a n)")[:, 0:NT * C].rearrange("p (t c) -> p t c", c=C)
        zt_ps = bank67.bitcast(FP16)
        h0_ps = bank67[:, :, 0:NB * C].rearrange("p a (j c) -> p a j c", c=C)
        zt0_ps = [[bank67[:, par, :].bitcast(FP16)[:, 0:NPE] for par in range(2)],
                  [bank03[:, 2 + par, :].bitcast(FP16)[:, 0:NPE] for par in range(2)]]
        ll_ps = bank67[:, 0, 0:NPE]
        f_ps = bank03
        u_ps = bank67
        d_ps = bank45
        warm_ps = bank45[:, 1, :]
        ll_last_ps = bank45[:, 1, 0:NPE]

        warm_ok = sem("warm_ok")
        ident_in, cst_in = sem("ident_in"), sem("cst_in")
        bias_in = sem("bias_in")
        w_in = sem("w_in")
        col_in = sem("col_in")
        fc_in = sem("fc_in")
        x_in = [sem(f"x_in{u}") for u in range(2)]
        out_done = sem("out_done")
        cleared = sem("cleared")
        ident16_ok = sem("ident16_ok")
        wb_ok = sem("wb_ok")
        wt_tr = sem("wt_tr")
        w_hi_ok, w_lo_ok = sem("w_hi_ok"), sem("w_lo_ok")
        x_tr = sem("x_tr")
        x_hi_ok, x_lo_ok = sem("x_hi_ok"), sem("x_lo_ok")
        xa0_tr, xa0_hi_ok = sem("xa0_tr"), sem("xa0_hi_ok")
        y_mm = sem("y_mm")
        y_ok = sem("y_ok")
        y_st = sem("y_st")
        bn_step = sem("bn_step")
        bn_rstd_ok = sem("bn_rstd_ok")
        bn_ok = sem("bn_ok")
        fct_tr = sem("fct_tr")
        fct_ok = sem("fct_ok")
        fold_mm = sem("fold_mm")
        folded_ok = sem("folded_ok")
        fold_ok = sem("fold_ok")
        h_ch_ok = sem("h_ch_ok")
        h_tr = sem("h_tr")
        h_ok = sem("h_ok")
        h_ch_odd_ok, h_even_tr = sem("h_ch_odd_ok"), sem("h_even_tr")
        st_even_ok, ln0_step = sem("st_even_ok"), sem("ln0_step")
        rstd0_ok = sem("rstd0_ok")
        off0_ok, z_odd_ok, z_hi_odd_ok = sem("off0_ok"), sem("z_odd_ok"), sem("z_hi_odd_ok")
        z_lo_even_ok, z_even_tr = sem("z_lo_even_ok"), sem("z_even_tr")
        st2_ok = sem("st2_ok")
        off_ok = sem("off_ok")
        ln_step = sem("ln_step")
        z_ok, z_hi_ok, z_lo_ok = sem("z_ok"), sem("z_hi_ok"), sem("z_lo_ok")
        z_tr = sem("z_tr")
        zt_hi_ok, zt_lo_ok = sem("zt_hi_ok"), sem("zt_lo_ok")
        s_mm = sem("s_mm")
        e_ok = sem("e_ok")
        o_mm = sem("o_mm")
        rden_ok, h2_ok, n_ok = sem("rden_ok"), sem("h2_ok"), sem("n_ok")
        q_ok, ll2_ok, ll_hi_ok, ll_lo_ok = sem("q_ok"), sem("ll2_ok"), sem("ll_hi_ok"), sem("ll_lo_ok")
        r_ok = sem("r_ok")
        ll_tr = sem("ll_tr")
        ll_t_ok = sem("ll_t_ok")
        ll_last_ok = sem("ll_last_ok")
        f_mm = sem("f_mm")
        g_ok = sem("g_ok")
        g_hi_dve, g_hi_act = sem("g_hi_dve"), sem("g_hi_act")
        g_lo_dve, g_lo_pool = sem("g_lo_dve"), sem("g_lo_pool")
        u_mm, u_ok, d_mm, o_ok = sem("u_mm"), sem("u_ok"), sem("d_mm"), sem("o_ok")

        block = ctx.enter_context(nc.Block())

        x_v = x.rearrange("b (p two) d -> b p (two d)", two=2)
        out_v = out.rearrange("b (p two) c -> b p (two c)", two=2)
        FULL = P * (NB - 1)

        def tile_cols(i):
            return (i // NB) * NP + (i % NB) * P

        def parts(table, b, k, listed):
            return sum((c in table[a]) == listed for a in range(b + 1) for c in range(KC if a < b else k + 1))

        @block.sync
        def _(sp):
            def load_x(b, u):
                sp.dma_start(xin[u][:, 0:NB - 1, 0:PF], x_v[b, 0:FULL, :].rearrange("(j p) n -> p j n", p=P))\
                  .then_inc(x_in[u], 16)
                sp.dma_start(xin[u][0:XROWS[-1], NB - 1, 0:PF], x_v[b, FULL:NPX, :]).then_inc(x_in[u], 16)
                for s in range(1, SPAN):
                    sp.dma_start(xin[u][:, 0:NB - 1, P + s * PB:P + (s + 1) * PB],
                                 x_v[b, s:s + FULL, P:PF].rearrange("(j p) n -> p j n", p=P)).then_inc(x_in[u], 16)
                at = x_v[b, FULL + 1:FULL + 2, P:PF].offset
                sp.dma_start(xin[u][0:ROWS[-1], NB - 1, PF:XW].rearrange("p (s n) -> p s n", n=PB),
                             bass.AP(tensor=x.tensor, offset=at, ap=[[PF, ROWS[-1]], [PF, SPAN - 1], [1, PB]]))\
                  .then_inc(x_in[u], 16)

            load_x(0, 0)
            load_x(1, 1)
            sp.dma_start(bias_c[:, :], tok_b.rearrange("(p a) -> p a", a=1)).then_inc(bias_in, 16)
            sp.wait_ge(x_tr, 1)
            load_x(2, 0)
            sp.dma_start(cst[:, :], consts[:, 0:2 * P]).then_inc(cst_in, 16)
            sp.dma_start(fc1_rows[:, :, :], fc1_w.rearrange("(k p) c -> p k c", p=P)).then_inc(fc_in, 16)
            sp.dma_start(fc2_rows[:, :], fc2_w).then_inc(fc_in, 16)
            sp.wait_ge(x_tr, 2)
            load_x(3, 1)
            for col, src in ((gamma_c, tok_gamma), (beta_c, tok_beta)):
                sp.dma_start(col[:, :], src.rearrange("(p a) -> p a", a=1)).then_inc(col_in, 16)
            for k in range(KC):
                sp.dma_start(fc1_bias[:, k:k + 1], fc1_b[P * k:P * k + P].rearrange("(p a) -> p a", a=1))\
                  .then_inc(col_in, 16)
            sp.dma_start(fc2_bias[0:CH, :], fc2_b.rearrange("(p a) -> p a", a=1)).then_inc(col_in, 16)
            with sp.Fori(2, B // 2) as i:
                for u in range(2):
                    sp.wait_ge(x_tr, 2 * i + u - 1)
                    load_x(2 * i + u, u)

            def store_blocks(b):
                sp.dma_start(out_v[b, 0:FULL, :].rearrange("(j p) n -> p j n", p=P),
                             r[:, b, 0:NB - 1, :, :].rearrange("p j t c -> p j (t c)")).then_inc(out_done, 16)

            def store_rest(b):
                sp.dma_start(out_v[b, FULL:NP, :],
                             r[0:ROWS[-1], b, NB - 1, :, :].rearrange("p t c -> p (t c)")).then_inc(out_done, 16)

            with sp.Fori(0, B - 1) as b:
                sp.wait_ge(o_ok, b + 1)
                store_blocks(b)
                store_rest(b)
            sp.wait_ge(o_ok, B)
            store_blocks(B - 1)
            sp.wait_ge(o_ok, B + 1)
            store_rest(B - 1)
            sp.wait_ge(out_done, 32 * B)

        @block.gpsimd
        def _(pool):
            pool.memset(shift_c[:, :], SHIFT).then_inc(cleared, 1)
            pool.memset(minus_half[:, :], -0.5)
            pool.memset(wpad[:, 0:D], 0.0)
            pool.memset(wpad[:, D + TAPS * D:], 0.0).then_inc(cleared, 1)
            for u in range(2):
                pool.memset(xa_hi[u][:, NPX:NPX + 1].bitcast(FP32), 0.0)
                pool.memset(xa_lo[u][:, NPX:NPX + 1].bitcast(FP32), 0.0)
                pool.memset(xb_hi[u][:, NP:NPE].bitcast(FP32), 0.0)
                pool.memset(xb_lo[u][:, NP:NPE].bitcast(FP32), 0.0)
            pool.memset(y[:, B * T:], 0.0)
            pool.memset(zt_hi[:, 2 * NPE:], 0.0)
            pool.memset(zt_lo[:, 2 * NPE:], 0.0)
            pool.memset(e[:, :, T:], 1.0)
            pool.memset(u_sb[0][:, NPE:], 0.0)
            pool.memset(u_sb[1][:, NPE:], 0.0).then_inc(r_ok, 1)
            for u in range(2):
                pool.memset(z[u][:, :, C:C + 1], 1.0).then_inc(cleared, 1)

            pool.wait_ge(bn_step, 2)
            pool.tensor_tensor(bn_rstd[:, :], bn_var[:, :], minus_half[:, 0:1], ALU.pow).then_inc(bn_rstd_ok, 1)

            pool.wait_ge(folded_ok, 1)
            pool.tensor_tensor(fc2_hl[:, :, 1, :], fc2_raw.rearrange("p (k c) -> p k c", c=CH),
                               fc2_hl[:, :, 0, :].bitcast(FP32), ALU.subtract)
            pool.tensor_tensor(fc1_lo[:, :], fc1_raw, fc1_hi[:, :].bitcast(FP32), ALU.subtract)\
                .then_inc(fold_ok, 1)

            pool.wait_ge(ln0_step, 4)
            pool.tensor_tensor(ln_rstd[:, NT:], ln_var[:, NT:], minus_half[:, :], ALU.pow).then_inc(rstd0_ok, 1)

            def residual(b):
                pool.wait_ge(n_ok, b + 1)
                pool.tensor_tensor(r[:, b, :, :, :].rearrange("p j t c -> p t j c"),
                                   h2[:, :, :].rearrange("p (t j) c -> p t j c", t=2),
                                   n[:, :, :].rearrange("p (t j) c -> p t j c", t=2), ALU.add).then_inc(r_ok, 1)

            with pool.Fori(0, B - 1) as b:
                residual(b)

            def split_g(b, u):
                if not (isinstance(b, int) and b < 2):
                    pool.wait_ge(u_mm, b - 1)
                for k in range(KC):
                    if k in LOW_ON_DVE[b]:
                        continue
                    if k in HIGH_ON_DVE[b]:
                        pool.wait_ge(g_hi_dve, parts(HIGH_ON_DVE, b, k, True))
                    else:
                        pool.wait_ge(g_hi_act, parts(HIGH_ON_DVE, b, k, False))
                    pool.tensor_tensor(g_lo[u][:, k, :], g[u][:, k, :],
                                       g_hi[u][:, k, :].bitcast(FP32), ALU.subtract).then_inc(g_lo_pool, 1)

            for b in range(B):
                split_g(b, b % 2)

        @block.tensor
        def _(pe):
            def keep_warm(products):
                for _ in range(products):
                    nc.tensor.matmul(warm_ps, warm[:, 0:P], warm[:, :], start=True, stop=True)

            def transpose_w(par):
                off = D * (1 - par)
                for s in range(SPAN):
                    nc.tensor.transpose(wt_ps[:, par, s, :], wpad[:, off + PF * s:off + PF * s + P], ident)
                if par == 0:
                    pe.wait_ge(wb_ok, 1)
                nc.tensor.transpose(wt_ps[0:SPAN * PB, par, SPAN, :],
                                    wb[:, par, :, :].rearrange("p s n -> p (s n)"), ident).then_inc(wt_tr, 1)

            def transpose_x(b, u, turn):
                pe.wait_ge(x_in[u], 16 * X_DMAS * (turn + 1))
                if not (isinstance(b, int) and b == 0):
                    pe.wait_ge(x_lo_ok, b)
                for j in range(NB):
                    last = nc.tensor.transpose(xa_ps[:, P * j:P * j + XROWS[j]], xin[u][0:XROWS[j], j, 0:P],
                                               ident[0:XROWS[j], 0:XROWS[j]])
                if isinstance(b, int) and b == 0:
                    last.then_inc(xa0_tr, 1)
                for j in range(NB):
                    last = nc.tensor.transpose(xb_ps[:, P * j:P * j + ROWS[j]], xin[u][0:ROWS[j], j, P:XW],
                                               ident[0:ROWS[j], 0:ROWS[j]])
                last.then_inc(x_tr, 1)

            def context_products(b, u):
                for par in range(2):
                    if not (isinstance(b, int) and b == 0):
                        pe.wait_ge(y_ok, 2 * b - 1 + par)
                    k = 0
                    for w, (xa, xb), ready in ((w_hi, (xa_hi, xb_hi), x_hi_ok), (w_hi, (xa_lo, xb_lo), x_lo_ok),
                                               (w_lo, (xa_hi, xb_hi), None)):
                        first = isinstance(b, int) and b == 0 and par == 0 and k == 0
                        if par == 0 and ready is not None and not first:
                            pe.wait_ge(ready, b + 1)
                        if ready is None and isinstance(b, int) and b == 0:
                            pe.wait_ge(w_lo_ok, par + 1)
                        for s in range(SPAN + 1):
                            if s < SPAN:
                                lhs, rhs = w[:, par, s, :], xa[u][:, s:s + NPE]
                            else:
                                if first:
                                    pe.wait_ge(x_hi_ok, 1)
                                lhs, rhs = w[0:SPAN * PB, par, s, :], xb[u][:, :]
                            last = nc.tensor.matmul(y_ps[:, par, 0:NPE], lhs, rhs,
                                                    start=(k == 0), stop=(k == 3 * (SPAN + 1) - 1))
                            k += 1
                        if first:
                            transpose_w(1)
                    last.then_inc(y_mm, 1)
                    if par == 0 and isinstance(b, int) and b == 0:
                        transpose_x(1, 1, 0)
                        pe.wait_ge(w_hi_ok, 2)

            pe.wait_ge(warm_ok, 1)
            keep_warm(WARM_START)
            pe.wait_ge(ident_in, 16)
            pe.wait_ge(w_in, 16)
            pe.wait_ge(cleared, 2)
            transpose_w(0)
            transpose_x(0, 0, 0)
            pe.wait_ge(w_hi_ok, 1)
            pe.wait_ge(xa0_hi_ok, 1)
            pe.wait_ge(cleared, 4)
            context_products(0, 0)
            with pe.Fori(0, B // 2 - 1) as i:
                transpose_x(2 * i + 2, 0, i + 1)
                context_products(2 * i + 1, 1)
                transpose_x(2 * i + 3, 1, i + 1)
                context_products(2 * i + 2, 0)
            context_products(B - 1, 1)

            pe.wait_ge(fc_in, 32)
            pe.wait_ge(cst_in, 16)
            for k in range(KC):
                last = nc.tensor.transpose(fc1t_ps[:, P * k:P * k + P], fc1_rows[:, k, :], ident)
            last.then_inc(ll_tr, 1)
            for k in range(KC):
                last = nc.tensor.transpose(fc2t_ps[:, CH * k:CH * k + CH], fc2_rows[:, P * k:P * k + P],
                                           ident[0:CH, 0:CH])
            last.then_inc(fct_tr, 1)
            pe.wait_ge(fct_ok, 1)
            nc.tensor.matmul(fold_ps, interp2, fc1_t[:, :], start=True, stop=True).then_inc(fold_mm, 1)

            def start_attention():
                pe.wait_ge(y_ok, 2 * B)
                keep_warm(WARM_NORM)
                pe.wait_ge(x_lo_ok, B)
                for par in range(2):
                    if par == 0:
                        pe.wait_ge(h_ch_ok, 1)
                    else:
                        pe.wait_ge(h_ch_odd_ok, 1)
                    for j in range(NB):
                        at = par * NP + P * j
                        last = nc.tensor.transpose(h0_ps[:, par, j, :], h_ch[:, at:at + P], ident)
                    last.then_inc(h_even_tr if par == 0 else h_tr, 1)
                keep_warm(WARM_Z)
                pe.wait_ge(ident16_ok, 1)
                pe.wait_ge(h_ok, 1)
                pe.wait_ge(folded_ok, 1)
                for part, zs in enumerate((z_hi, z_lo)):
                    for par in range(2):
                        if part == 0:
                            pe.wait_ge(z_hi_ok if par == 0 else z_hi_odd_ok, 1)
                        else:
                            pe.wait_ge(z_lo_even_ok if par == 0 else z_lo_ok, 1)
                        for j in range(NB):
                            rows = min(P, NPE - P * j)
                            last = nc.tensor.transpose(zt0_ps[part][par][:, P * j:P * j + rows],
                                                       zs[0:rows, NB * par + j, :],
                                                       ident16[0:rows, 0:rows])
                        last.then_inc(z_even_tr if par == 0 else z_tr, 1)

            def transpose_h(b):
                pe.wait_ge(h_ch_ok, b + 1)
                pe.wait_ge(zt_hi_ok, b)
                pe.wait_ge(zt_lo_ok, b)
                if not (isinstance(b, int) and b == 1):
                    pe.wait_ge(ll_t_ok, b - 1)
                for i in range(NT):
                    at = tile_cols(i)
                    last = nc.tensor.transpose(h_ps[:, i, :], h_ch[:, at:at + P], ident)
                last.then_inc(h_tr, 1)

            def transpose_z(b):
                pe.wait_ge(z_hi_ok, b + 1)
                for part, zs in enumerate((z_hi, z_lo)):
                    if part:
                        pe.wait_ge(z_lo_ok, b + 1)
                    for i in range(NT):
                        par, j = i // NB, i % NB
                        rows = min(P, NPE - P * j)
                        at = par * NPE + P * j
                        last = nc.tensor.transpose(zt_ps[:, part, at:at + rows], zs[0:rows, i, :],
                                                   ident16[0:rows, 0:rows])
                    last.then_inc(z_tr, 1)

            def transpose_ll(b, dst):
                pe.wait_ge(ll_lo_ok, b + 1)
                for j in range(NB):
                    rows = min(P, NPE - P * j)
                    last = nc.tensor.transpose(dst[:, P * j:P * j + rows],
                                               ll_hl[0:rows, j, :, :].rearrange("p a c -> p (a c)").bitcast(FP32),
                                               ident[0:rows, 0:rows])
                last.then_inc(ll_tr, 1)

            def scores(b, i):
                at = (i // NB) * NPE + (i % NB) * P
                if not (isinstance(b, int) and b == 0 and i < 2):
                    pe.wait_ge(e_ok, NT * b + i - 1)
                ahead = isinstance(b, int) and b == 0 and i == 0
                if ahead:
                    for par in range(2):
                        nc.tensor.matmul(s_ps[:, 0, par, 0:NP], zt_hi[:, 0:P],
                                         zt_hi[:, par * NPE:par * NPE + NP], start=True, stop=False)
                    pe.wait_ge(zt_lo_ok, 1)
                for par in range(2):
                    cols = slice(par * NPE, par * NPE + NP)
                    dst = s_ps[:, i % 2, par, 0:NP]
                    if not ahead:
                        nc.tensor.matmul(dst, zt_hi[:, at:at + P], zt_hi[:, cols], start=True, stop=False)
                    nc.tensor.matmul(dst, zt_hi[:, at:at + P], zt_lo[:, cols], start=False, stop=False)
                    last = nc.tensor.matmul(dst, zt_lo[:, at:at + P], zt_hi[:, cols], start=False, stop=True)
                last.then_inc(s_mm, 1)

            def attend(b, zu, i):
                par, j = i // NB, i % NB
                if j == 0:
                    if isinstance(b, int) and b == 0:
                        pe.wait_ge(y_ok, 2 * B)
                    else:
                        pe.wait_ge(h2_ok, 2 * b - 1 + par)
                for k in range(NT):
                    if i == 0:
                        pe.wait_ge(e_ok, NT * b + k + 1)
                    rows = ROWS[k % NB]
                    last = nc.tensor.matmul(o_ps[:, par, j * (C + 1):(j + 1) * (C + 1)],
                                            e[0:rows, k, tile_cols(i):tile_cols(i) + P],
                                            z[zu][0:rows, k, :], start=(k == 0), stop=(k == NT - 1))
                if j == NB - 1:
                    last.then_inc(o_mm, 1)

            def hidden(b):
                if b == B - 1:
                    pe.wait_ge(ll_last_ok, 1)
                else:
                    pe.wait_ge(ll_t_ok, b + 2)
                for k in range(KC):
                    if isinstance(b, int) and b == 0:
                        pe.wait_ge(e_ok, B * NT)
                    else:
                        pe.wait_ge(g_ok, KC * b - (KC - 1) + k)
                    rhs = ll_t[:, b, :]
                    nc.tensor.matmul(f_ps[:, k, 0:NPE], fc1_hi[:, P * k:P * k + P], rhs, start=True, stop=False)
                    nc.tensor.matmul(f_ps[:, k, 0:NPE], fc1_lo[:, P * k:P * k + P], rhs, start=False, stop=True)\
                      .then_inc(f_mm, 1)

            def project(b, u):
                if isinstance(b, int) and b < 2:
                    pe.wait_ge(ll_t_ok, B)
                else:
                    pe.wait_ge(u_ok, b - 1)
                for k in range(KC):
                    if k in HIGH_ON_DVE[b]:
                        pe.wait_ge(g_hi_dve, parts(HIGH_ON_DVE, b, k, True))
                    else:
                        pe.wait_ge(g_hi_act, parts(HIGH_ON_DVE, b, k, False))
                    lhs = fc2_hl[:, k, :, :].rearrange("p a c -> p (a c)")
                    nc.tensor.matmul(u_ps[:, u, 0:NPE], lhs, g_hi[u][:, k, :], start=(k == 0), stop=False)
                    if k in LOW_ON_DVE[b]:
                        pe.wait_ge(g_lo_dve, parts(LOW_ON_DVE, b, k, True))
                    else:
                        pe.wait_ge(g_lo_pool, parts(LOW_ON_DVE, b, k, False))
                    last = nc.tensor.matmul(u_ps[:, u, 0:NPE], lhs, g_lo[u][:, k, :], start=False, stop=(k == KC - 1))
                last.then_inc(u_mm, 1)

            def attention(b, u, first=False, last=False):
                pe.wait_ge(zt_hi_ok, b + 1)
                if not first:
                    pe.wait_ge(zt_lo_ok, b + 1)
                scores(b, 0)
                scores(b, 1)
                if not last:
                    transpose_h(b + 1)
                for i in range(2, NT):
                    scores(b, i)
                attend(b, u, 0)
                attend(b, u, 1)
                if last:
                    pe.wait_ge(fold_ok, 1)
                    hidden(0)
                attend(b, u, 2)
                if last:
                    transpose_ll(b - 1, ll_ps)
                attend(b, u, 3)
                if last:
                    hidden(1)
                else:
                    pe.wait_ge(h_ok, b + 2)
                    transpose_z(b + 1)
                attend(b, u, 4)
                if last:
                    project(0, 0)
                    hidden(2)
                elif not first:
                    pe.wait_ge(zt_hi_ok, b + 2)
                    transpose_ll(b - 1, ll_ps)
                attend(b, u, 5)

            start_attention()
            attention(0, 0, first=True)
            with pe.Fori(0, B // 2 - 1) as i:
                attention(2 * i + 1, 1)
                attention(2 * i + 2, 0)
            attention(B - 1, 1, last=True)

            def spread(b, u):
                pe.wait_ge(u_ok, b + 1)
                if isinstance(b, int) and b == 0:
                    pe.wait_ge(h2_ok, 2 * B)
                elif b > 1:
                    pe.wait_ge(o_ok, b - 1)
                for j in range(NB):
                    last = nc.tensor.matmul(d_ps[:, u, C * j:C * j + C], u_sb[u][:, P * j:P * j + P], dup,
                                            start=True, stop=True)
                last.then_inc(d_mm, 1)

            project(1, 1)
            hidden(3)
            spread(0, 0)
            project(2, 0)
            hidden(4)
            spread(1, 1)
            project(3, 1)
            hidden(5)
            spread(2, 0)
            project(4, 0)
            hidden(6)
            pe.wait_ge(o_ok, 2)
            transpose_ll(B - 1, ll_last_ps)
            project(5, 1)
            pe.wait_ge(ll_last_ok, 1)
            spread(3, 1)
            hidden(7)
            spread(4, 0)
            project(6, 0)
            spread(5, 1)
            project(7, 1)
            spread(6, 0)
            spread(7, 1)

        @block.scalar
        def _(act):
            act.dma_start(ident, consts[:, 2 * P:3 * P]).then_inc(ident_in, 16)
            act.dma_start(wpad[:, D:D + TAPS * D], tok_w).then_inc(w_in, 16)
            act.wait_ge(cleared, 1)
            nc.scalar.activation(table_c[:, :], shift_c[:, :], ACT.Exp)
            nc.scalar.activation(ln_off[:, 0:1], shift_c[:, :], ACT.Copy).then_inc(ll_t_ok, 1)

            def weights_hi(par):
                act.wait_ge(wt_tr, par + 1)
                nc.scalar.activation(w_hi[:, par, 0:SPAN, :], wt_ps[:, par, 0:SPAN, :], ACT.Copy)
                nc.scalar.activation(w_hi[0:SPAN * PB, par, SPAN, :], wt_ps[0:SPAN * PB, par, SPAN, :], ACT.Copy)\
                  .then_inc(w_hi_ok, 1)

            def frames_hi(b, u):
                if isinstance(b, int) and b == 0:
                    act.wait_ge(xa0_tr, 1)
                    nc.scalar.activation(xa_hi[u][:, 0:NPX], xa_ps, ACT.Copy).then_inc(xa0_hi_ok, 1)
                    act.wait_ge(x_tr, 1)
                else:
                    act.wait_ge(x_tr, b + 1)
                    if not (isinstance(b, int) and b == 1):
                        act.wait_ge(y_mm, 2 * b - 2)
                    nc.scalar.activation(xa_hi[u][:, 0:NPX], xa_ps, ACT.Copy)
                nc.scalar.activation(xb_hi[u][:, 0:NP], xb_ps, ACT.Copy).then_inc(x_hi_ok, 1)

            def relu(b):
                for par in range(2):
                    act.wait_ge(y_mm, 2 * b + par + 1)
                    nc.scalar.activation(y[:, bass.ds(b * T + par * NP, NP)], y_ps[:, par, 0:NP], ACT.Relu,
                                         bias=bias_c[:, :]).then_inc(y_ok, 1)

            weights_hi(0)
            frames_hi(0, 0)
            weights_hi(1)
            frames_hi(1, 1)
            act.wait_ge(bias_in, 16)
            relu(0)
            with act.Fori(0, B // 2 - 1) as i:
                frames_hi(2 * i + 2, 0)
                relu(2 * i + 1)
                frames_hi(2 * i + 3, 1)
                relu(2 * i + 2)
            relu(B - 1)

            nc.scalar.activation(ident16[:, :], ident, ACT.Copy).then_inc(ident16_ok, 1)
            act.wait_ge(col_in, 16 * (3 + KC))
            act.wait_ge(fct_tr, 1)
            nc.scalar.activation(fc1_t[:, :], fc1t_ps, ACT.Copy).then_inc(fct_ok, 1)
            nc.scalar.activation(fc2_hl[:, :, 0, :], fc2t_ps.rearrange("p (k c) -> p k c", c=CH), ACT.Copy)
            nc.scalar.activation(fc2_raw, fc2t_ps, ACT.Copy)

            def normalise_channels(b):
                act.wait_ge(h_tr, b)
                nc.scalar.activation(h_ch[:, :], y[:, bass.ds(b * T, TPAD)], ACT.Identity,
                                     bias=bn_shift[:, :], scale=bn_scale[:, :]).then_inc(h_ch_ok, 1)

            def copy_h(b, u):
                act.wait_ge(h_tr, b + 1)
                if not (isinstance(b, int) and b < 2):
                    act.wait_ge(h2_ok, 2 * b - 2)
                nc.scalar.activation(h[u][:, :, :], h_ps, ACT.Copy).then_inc(h_ok, 1)

            def exponentials(b, i):
                act.wait_ge(s_mm, NT * b + i + 1)
                if i == 0 and not (isinstance(b, int) and b == 0):
                    act.wait_ge(o_mm, 2 * b)
                nc.scalar.activation(e[:, i, 0:T].rearrange("p (a n) -> p a n", a=2), s_ps[:, i % 2, :, 0:NP],
                                     ACT.Exp, bias=shift_c[:, :]).then_inc(e_ok, 1)

            def copy_zt_hi(b):
                act.wait_ge(z_tr, 2 * b + 1)
                if not (isinstance(b, int) and b == 0):
                    act.wait_ge(s_mm, NT * b)
                nc.scalar.activation(zt_hi[:, 0:2 * NPE], zt_ps[:, 0, 0:2 * NPE], ACT.Copy).then_inc(zt_hi_ok, 1)

            def second_norm(b):
                act.wait_ge(off_ok, b + 1)
                act.wait_ge(r_ok, b + 1)
                for i in range(NT):
                    last = nc.scalar.activation(n[:, i, :], h2[:, i, :], ACT.Identity,
                                                bias=ln_off[:, i:i + 1], scale=ln_rstd[:, i:i + 1])
                last.then_inc(n_ok, 1)

            def copy_ll(b, src):
                act.wait_ge(ll_tr, b + 2)
                nc.scalar.activation(ll_t[:, b, :], src, ACT.Copy).then_inc(ll_t_ok, 1)

            def attention(b, u, first=False, last=False):
                exponentials(b, 0)
                exponentials(b, 1)
                if not last:
                    copy_h(b + 1, 1 - u)
                for i in range(2, NT):
                    exponentials(b, i)
                if not last and not (isinstance(b, int) and b == B - 2):
                    normalise_channels(b + 2)
                if not first:
                    second_norm(b - 1)
                if not last:
                    copy_zt_hi(b + 1)
                if last:
                    gelu(0, 0)
                if not first:
                    copy_ll(b - 1, ll_ps)
                if last:
                    gelu(1, 1)

            def gelu(b, u):
                for k in range(KC + 1):
                    if k < KC:
                        act.wait_ge(f_mm, KC * b + k + 1)
                        if k == 0 and b >= 2:
                            act.wait_ge(g_lo_dve, parts(LOW_ON_DVE, b - 2, KC - 1, True))
                            act.wait_ge(g_lo_pool, parts(LOW_ON_DVE, b - 2, KC - 1, False))
                        nc.scalar.activation(g[u][:, k, :], f_ps[:, k, 0:NPE], ACT.Gelu,
                                             bias=fc1_bias[:, k:k + 1]).then_inc(g_ok, 1)
                    if k == 1 and b >= 2:
                        act.wait_ge(u_mm, b - 1)
                    if k > 0 and k - 1 not in HIGH_ON_DVE[b]:
                        act.wait_ge(g_ok, KC * b + k)
                        nc.scalar.activation(g_hi[u][:, k - 1, :], g[u][:, k - 1, :], ACT.Copy)\
                          .then_inc(g_hi_act, 1)

            def start_attention():
                act.wait_ge(bn_ok, 2)
                nc.scalar.activation(h_ch[:, 0:NB * P], y[:, 0:NB * P], ACT.Identity,
                                     bias=bn_shift[:, :], scale=bn_scale[:, :]).then_inc(h_ch_ok, 1)
                act.wait_ge(fold_mm, 1)
                nc.scalar.activation(fc1_hi[:, :], fold_ps, ACT.Copy)
                nc.scalar.activation(fc1_raw, fold_ps, ACT.Copy).then_inc(folded_ok, 1)
                for par in range(2):
                    if par == 0:
                        act.wait_ge(st_even_ok, 1)
                    else:
                        act.wait_ge(st2_ok, 1)
                    last = nc.scalar.activation(h[0][:, NB * par:NB * par + NB, :], h0_ps[:, par, :, :], ACT.Copy)
                last.then_inc(h_ok, 1)
                normalise_channels(1)
                act.wait_ge(h_ok, 1)
                act.wait_ge(off0_ok, 1)
                for i in range(NB, NT):
                    last = nc.scalar.activation(z[0][:, i, 0:C], h[0][:, i, :], ACT.Identity,
                                                bias=ln_off[:, i:i + 1], scale=ln_rstd[:, NT + i:NT + i + 1])
                last.then_inc(z_odd_ok, 1)
                act.wait_ge(z_odd_ok, 1)
                nc.scalar.activation(z_hi[:, NB:NT, :], z[0][:, NB:NT, 0:C], ACT.Copy).then_inc(z_hi_odd_ok, 1)
                act.wait_ge(z_even_tr, 1)
                nc.scalar.activation(zt_hi[:, 0:NPE], zt0_ps[0][0], ACT.Copy)
                act.wait_ge(z_tr, 1)
                nc.scalar.activation(zt_hi[:, NPE:2 * NPE], zt0_ps[0][1], ACT.Copy).then_inc(zt_hi_ok, 1)

            start_attention()
            attention(0, 0, first=True)
            with act.Fori(0, B // 2 - 2) as i:
                attention(2 * i + 1, 1)
                attention(2 * i + 2, 0)
            attention(B - 3, 1)
            attention(B - 2, 0)
            attention(B - 1, 1, last=True)
            gelu(2, 0)
            gelu(3, 1)
            gelu(4, 0)
            second_norm(B - 1)
            gelu(5, 1)
            gelu(6, 0)
            gelu(7, 1)

        @block.vector
        def _(dve):
            nc.vector.memset(warm[:, :], 0.0).then_inc(warm_ok, 1)
            nc.vector.memset(fc2_bias[CH:, :], 0.0)
            dve.wait_ge(w_in, 16)
            dve.wait_ge(cleared, 2)
            for par in range(2):
                at = D * (1 - par) + P
                last = nc.vector.tensor_copy(
                    wb[:, par, :, :], wpad[:, at:at + SPAN * PF].rearrange("p (s n) -> p s n", n=PF)[:, :, 0:PB])
            last.then_inc(wb_ok, 1)
            def frames_lo(b, u):
                if isinstance(b, int) and b == 0:
                    dve.wait_ge(xa0_hi_ok, 1)
                else:
                    dve.wait_ge(x_hi_ok, b + 1)
                nc.vector.tensor_tensor(xa_lo[u][:, 0:NPX], xa_ps, xa_hi[u][:, 0:NPX].bitcast(FP32), ALU.subtract)
                if isinstance(b, int) and b == 0:
                    dve.wait_ge(x_hi_ok, 1)
                nc.vector.tensor_tensor(xb_lo[u][:, 0:NP], xb_ps, xb_hi[u][:, 0:NP].bitcast(FP32), ALU.subtract)\
                  .then_inc(x_lo_ok, 1)

            def channel_stats(b):
                for par in range(2):
                    dve.wait_ge(y_ok, 2 * b + par + 1)
                    nc.vector.bn_stats(bn[:, bass.ds(2 * b + par, 1), :].rearrange("p a s -> p (a s)"),
                                       y[:, bass.ds(b * T + par * NP, NP)]).then_inc(y_st, 1)

            def weights_lo(par):
                dve.wait_ge(w_hi_ok, par + 1)
                nc.vector.tensor_tensor(w_lo[:, par, 0:SPAN, :], wt_ps[:, par, 0:SPAN, :],
                                        w_hi[:, par, 0:SPAN, :].bitcast(FP32), ALU.subtract)
                nc.vector.tensor_tensor(w_lo[0:SPAN * PB, par, SPAN, :], wt_ps[0:SPAN * PB, par, SPAN, :],
                                        w_hi[0:SPAN * PB, par, SPAN, :].bitcast(FP32), ALU.subtract)\
                  .then_inc(w_lo_ok, 1)

            frames_lo(0, 0)
            weights_lo(0)
            weights_lo(1)
            frames_lo(1, 1)
            channel_stats(0)
            with dve.Fori(0, B // 2 - 1) as i:
                frames_lo(2 * i + 2, 0)
                channel_stats(2 * i + 1)
                frames_lo(2 * i + 3, 1)
                channel_stats(2 * i + 2)
            channel_stats(B - 1)

            I32 = mybir.dt.int32

            dve.wait_ge(y_st, 2 * B)
            dve.wait_ge(col_in, 16 * (3 + KC))
            nc.vector.bn_aggr(bn_mv[:, :], bn[:, :, :].rearrange("p a s -> p (a s)")).then_inc(bn_step, 1)
            dve.wait_ge(bn_step, 1)
            nc.vector.tensor_scalar(bn_var[:, :], bn_mv[:, 1:2], EPS, None, ALU.add).then_inc(bn_step, 1)
            nc.vector.tensor_scalar(bn_mean_neg[:, :], bn_mv[:, 0:1], -1.0, None, ALU.mult)
            dve.wait_ge(bn_rstd_ok, 1)
            nc.vector.tensor_tensor(bn_scale[:, :], bn_rstd[:, :], gamma_c[:, :], ALU.mult).then_inc(bn_ok, 1)
            dve.wait_ge(bn_ok, 1)
            nc.vector.tensor_scalar(bn_shift[:, :], bn_scale[:, :], bn_mean_neg[:, :], beta_c[:, :],
                                    ALU.mult, ALU.add).then_inc(bn_ok, 1)

            def rsqrt(out, v, y, scale, done, at):
                def link(instruction):
                    nonlocal at
                    at = at + 1
                    instruction.then_inc(done, 1)
                    dve.wait_ge(done, at)

                A1, B1 = 0.703952253, 0.703952253 * 2.38924456
                link(nc.vector.tensor_scalar(y[0].bitcast(I32), v.bitcast(I32), 1, None, ALU.logical_shift_right))
                link(nc.vector.tensor_scalar(y[1].bitcast(I32), y[0].bitcast(I32), -1.0, float(0x5F1FFFF9),
                                             ALU.mult, ALU.add))
                link(nc.vector.tensor_tensor(y[0], y[1], y[1], ALU.mult))
                link(nc.vector.scalar_tensor_tensor(y[2], y[0], -A1, v, ALU.mult, ALU.mult))
                link(nc.vector.scalar_tensor_tensor(y[3], y[2], B1, y[1], ALU.add, ALU.mult))
                link(nc.vector.tensor_tensor(y[0], y[3], y[3], ALU.mult))
                link(nc.vector.tensor_tensor(y[4], y[0], v, ALU.mult))
                link(nc.vector.tensor_scalar(y[5], y[4], 0.375 * scale, -1.25 * scale, ALU.mult, ALU.add))
                link(nc.vector.tensor_tensor(y[6], y[5], y[4], ALU.mult))
                link(nc.vector.scalar_tensor_tensor(out, y[6], 1.875 * scale, y[3], ALU.add, ALU.mult))

            def add_attention(b, u):
                for par in range(2):
                    dve.wait_ge(o_mm, 2 * b + par + 1)
                    ov = o_ps[:, par, 0:NB * (C + 1)].rearrange("p (j c) -> p j c", c=C + 1)
                    nc.vector.reciprocal(rden[:, NB * par:NB * par + NB], ov[:, :, C]).then_inc(rden_ok, 1)
                    dve.wait_ge(rden_ok, 2 * b + par + 1)
                    if par == 0:
                        dve.wait_ge(r_ok, b + 1)
                    for j in range(NB):
                        i = NB * par + j
                        last = nc.vector.scalar_tensor_tensor(h2[:, i, :], ov[:, j, 0:C], rden[:, i:i + 1],
                                                              h[u][:, i, :], ALU.mult, ALU.add)
                    last.then_inc(h2_ok, 1)
                dve.wait_ge(h2_ok, 2 * b + 2)
                for i in range(NT):
                    last = nc.vector.bn_stats(ln[:, i, :], h2[:, i, :])
                last.then_inc(st2_ok, 1)

            def first_stats(b, u):
                dve.wait_ge(h_ok, b + 1)
                for i in range(NT):
                    last = nc.vector.bn_stats(ln[:, NT + i, :], h[u][:, i, :])
                last.then_inc(st2_ok, 1)

            def layer_norms(lo, hi, turn, stats):
                at = LN_STEPS * turn
                dve.wait_ge(st2_ok, stats)
                nc.vector.tensor_tensor(ln_dif[:, lo:hi], ln[:, lo:hi, 1], ln[:, lo:hi, 4], ALU.subtract)\
                  .then_inc(ln_step, 1)
                nc.vector.tensor_tensor(ln_sum[:, lo:hi, :], ln[:, lo:hi, 1:3], ln[:, lo:hi, 4:6], ALU.add)\
                  .then_inc(ln_step, 1)
                dve.wait_ge(ln_step, at + 1)
                nc.vector.scalar_tensor_tensor(ln_sq[:, lo:hi], ln_dif[:, lo:hi], C / 4.0, ln_dif[:, lo:hi],
                                               ALU.mult, ALU.mult).then_inc(ln_step, 1)
                dve.wait_ge(ln_step, at + 3)
                nc.vector.scalar_tensor_tensor(ln_var[:, lo:hi], ln_sq[:, lo:hi], C * EPS, ln_sum[:, lo:hi, 1],
                                               ALU.add, ALU.add).then_inc(ln_step, 1)
                nc.vector.tensor_scalar(ln_mean[:, lo:hi], ln_sum[:, lo:hi, 0], 0.5, None, ALU.mult)\
                  .then_inc(ln_step, 1)
                dve.wait_ge(ln_step, at + 5)
                rsqrt(ln_rstd[:, lo:hi], ln_var[:, lo:hi], [ln_y[:, k, lo:hi] for k in range(7)],
                      float(C) ** 0.5, ln_step, at + 5)

            def second_offsets():
                nc.vector.scalar_tensor_tensor(ln_off[:, :], ln_mean[:, 0:NT], -1.0, ln_rstd[:, 0:NT],
                                               ALU.mult, ALU.mult).then_inc(off_ok, 1)

            def band(b):
                dve.wait_ge(n_ok, b + 1)
                nc.vector.tensor_tensor(q[:, :, :], n[:, 0:NB, :], n[:, NB:NT, :], ALU.add).then_inc(q_ok, 1)
                dve.wait_ge(q_ok, b + 1)
                qv = q[:, :, :].rearrange("p j (c two) -> p j c two", two=2)
                nc.vector.tensor_tensor(ll2[:, :, :], qv[:, :, :, 0], qv[:, :, :, 1], ALU.add).then_inc(ll2_ok, 1)
                dve.wait_ge(ll2_ok, b + 1)
                dve.wait_ge(ll_tr, b + 1)
                nc.vector.tensor_scalar(ll_hl[:, :, 0, :], ll2[:, :, :], 0.5, None, ALU.mult).then_inc(ll_hi_ok, 1)
                dve.wait_ge(ll_hi_ok, b + 1)
                nc.vector.scalar_tensor_tensor(ll_hl[:, :, 1, :], ll2[:, :, :], 0.5,
                                               ll_hl[:, :, 0, :].bitcast(FP32), ALU.mult, ALU.subtract)\
                  .then_inc(ll_lo_ok, 1)

            def first_norm(b, u):
                if not (isinstance(b, int) and b < 2):
                    dve.wait_ge(o_mm, 2 * b - 2)
                for i in range(NT):
                    last = nc.vector.tensor_scalar(z[u][:, i, 0:C], h[u][:, i, :], ln_mean[:, NT + i:NT + i + 1],
                                                   ln_rstd[:, NT + i:NT + i + 1], ALU.subtract, ALU.mult)
                last.then_inc(z_ok, 1)
                dve.wait_ge(z_ok, b + 1)
                if not (isinstance(b, int) and b == 0):
                    dve.wait_ge(z_tr, 2 * b)
                nc.vector.tensor_copy(z_hi[:, :, :], z[u][:, :, 0:C]).then_inc(z_hi_ok, 1)
                dve.wait_ge(z_hi_ok, b + 1)
                nc.vector.tensor_tensor(z_lo[:, :, :], z[u][:, :, 0:C], z_hi[:, :, :], ALU.subtract)\
                  .then_inc(z_lo_ok, 1)

            def copy_zt_lo(b):
                if not (isinstance(b, int) and b == 0):
                    dve.wait_ge(s_mm, NT * b)
                dve.wait_ge(z_tr, 2 * b + 2)
                nc.vector.tensor_copy(zt_lo[:, 0:2 * NPE], zt_ps[:, 1, 0:2 * NPE]).then_inc(zt_lo_ok, 1)

            def attention(b, u, first=False, last=False):
                if not first:
                    add_attention(b - 1, 1 - u)
                if not last:
                    first_stats(b + 1, 1 - u)
                layer_norms(NT if first else 0, NT if last else 2 * NT, b, 2 * b + 2 if not last else 2 * B - 1)
                if not first:
                    second_offsets()
                if not last:
                    first_norm(b + 1, 1 - u)
                if not first:
                    band(b - 1)
                if not last:
                    copy_zt_lo(b + 1)

            def start_attention():
                nc.vector.tensor_scalar(h_ch[:, NB * P:], y[:, NB * P:TPAD], bn_scale[:, :], bn_shift[:, :],
                                        ALU.mult, ALU.add).then_inc(h_ch_odd_ok, 1)
                for par in range(2):
                    dve.wait_ge(h_even_tr if par == 0 else h_tr, 1)
                    for j in range(NB):
                        last = nc.vector.bn_stats(ln[:, NT + NB * par + j, :], h0_ps[:, par, j, :])
                    last.then_inc(st_even_ok if par == 0 else st2_ok, 1)
                dve.wait_ge(st2_ok, 1)
                nc.vector.tensor_tensor(ln_dif[:, NT:], ln[:, NT:, 1], ln[:, NT:, 4], ALU.subtract)
                nc.vector.tensor_tensor(ln_sum[:, NT:, :], ln[:, NT:, 1:3], ln[:, NT:, 4:6], ALU.add)\
                  .then_inc(ln0_step, 1)
                dve.wait_ge(ln0_step, 1)
                nc.vector.scalar_tensor_tensor(ln_sq[:, NT:], ln_dif[:, NT:], 0.25, ln_dif[:, NT:],
                                               ALU.mult, ALU.mult).then_inc(ln0_step, 1)
                nc.vector.tensor_scalar(ln_y[:, 0, NT:], ln_sum[:, NT:, 1], 1.0 / C, EPS, ALU.mult, ALU.add)\
                  .then_inc(ln0_step, 1)
                dve.wait_ge(ln0_step, 3)
                nc.vector.tensor_tensor(ln_var[:, NT:], ln_y[:, 0, NT:], ln_sq[:, NT:], ALU.add).then_inc(ln0_step, 1)
                nc.vector.tensor_scalar(ln_mean[:, NT:], ln_sum[:, NT:, 0], 0.5, None, ALU.mult).then_inc(ln0_step, 1)
                dve.wait_ge(ln0_step, 5)
                dve.wait_ge(rstd0_ok, 1)
                nc.vector.scalar_tensor_tensor(ln_off[:, :], ln_mean[:, NT:], -1.0, ln_rstd[:, NT:],
                                               ALU.mult, ALU.mult).then_inc(off0_ok, 1)
                dve.wait_ge(h_ok, 1)
                for i in range(NB):
                    last = nc.vector.tensor_scalar(z[0][:, i, 0:C], h[0][:, i, :], ln_mean[:, NT + i:NT + i + 1],
                                                   ln_rstd[:, NT + i:NT + i + 1], ALU.subtract, ALU.mult)
                last.then_inc(z_ok, 1)
                dve.wait_ge(z_ok, 1)
                nc.vector.tensor_copy(z_hi[:, 0:NB, :], z[0][:, 0:NB, 0:C]).then_inc(z_hi_ok, 1)
                dve.wait_ge(z_hi_ok, 1)
                nc.vector.tensor_tensor(z_lo[:, 0:NB, :], z[0][:, 0:NB, 0:C], z_hi[:, 0:NB, :], ALU.subtract)\
                  .then_inc(z_lo_even_ok, 1)
                dve.wait_ge(z_hi_odd_ok, 1)
                nc.vector.tensor_tensor(z_lo[:, NB:NT, :], z[0][:, NB:NT, 0:C], z_hi[:, NB:NT, :], ALU.subtract)\
                  .then_inc(z_lo_ok, 1)
                dve.wait_ge(z_even_tr, 2)
                nc.vector.tensor_copy(zt_lo[:, 0:NPE], zt0_ps[1][0])
                dve.wait_ge(z_tr, 2)
                nc.vector.tensor_copy(zt_lo[:, NPE:2 * NPE], zt0_ps[1][1]).then_inc(zt_lo_ok, 1)

            dve.wait_ge(bn_ok, 2)
            start_attention()
            attention(0, 0, first=True)
            with dve.Fori(0, B // 2 - 1) as i:
                attention(2 * i + 1, 1)
                attention(2 * i + 2, 0)
            attention(B - 1, 1, last=True)

            def split_g(b, u):
                if b >= 2:
                    dve.wait_ge(u_mm, b - 1)
                for k in HIGH_ON_DVE[b]:
                    dve.wait_ge(g_ok, KC * b + k + 1)
                    nc.vector.tensor_copy(g_hi[u][:, k, :], g[u][:, k, :]).then_inc(g_hi_dve, 1)
                    if k in LOW_ON_DVE[b]:
                        dve.wait_ge(g_hi_dve, parts(HIGH_ON_DVE, b, k, True))
                        nc.vector.tensor_tensor(g_lo[u][:, k, :], g[u][:, k, :], g_hi[u][:, k, :].bitcast(FP32),
                                                ALU.subtract).then_inc(g_lo_dve, 1)

            def band_change(b, u):
                dve.wait_ge(u_mm, b + 1)
                if b >= 2:
                    dve.wait_ge(d_mm, b - 1)
                if b == B - 1:
                    dve.wait_ge(ll_last_ok, 1)
                else:
                    dve.wait_ge(ll_t_ok, b + 2)
                nc.vector.scalar_tensor_tensor(u_sb[u][:, 0:NPE], u_ps[:, u, 0:NPE], fc2_bias[:, :],
                                               ll_t[:, b, :].bitcast(FP32), ALU.add, ALU.subtract)\
                  .then_inc(u_ok, 1)

            def finish(b, u):
                dve.wait_ge(d_mm, b + 1)
                dve.wait_ge(r_ok, b + 2)
                dv = d_ps[:, u, 0:NB * C].rearrange("p (j c) -> p j c", c=C)
                for blocks in ((slice(0, NB),) if b < B - 1 else (slice(0, NB - 1), slice(NB - 1, NB))):
                    rv = r[:, b, blocks, :, :]
                    change = dv[:, blocks, :].unsqueeze(2).broadcast_to(rv.shape)
                    nc.vector.tensor_tensor(rv, change, rv, ALU.add).then_inc(o_ok, 1)

            split_g(0, 0)
            split_g(1, 1)
            band_change(0, 0)
            add_attention(B - 1, 1)
            band_change(1, 1)
            layer_norms(0, NT, B, 2 * B)
            second_offsets()
            split_g(3, 1)
            band_change(2, 0)
            finish(0, 0)
            finish(1, 1)
            split_g(4, 0)
            band_change(3, 1)
            band(B - 1)
            finish(2, 0)
            split_g(5, 1)
            dve.wait_ge(ll_tr, B + 1)
            nc.vector.tensor_copy(ll_t[:, B - 1, :], ll_last_ps).then_inc(ll_last_ok, 1)
            band_change(4, 0)
            nc.vector.tensor_tensor(r[:, B - 1, :, :, :].rearrange("p j t c -> p t j c"),
                                    h2[:, :, :].rearrange("p (t j) c -> p t j c", t=2),
                                    n[:, :, :].rearrange("p (t j) c -> p t j c", t=2), ALU.add).then_inc(r_ok, 1)
            finish(3, 1)
            split_g(6, 0)
            band_change(5, 1)
            finish(4, 0)
            split_g(7, 1)
            band_change(6, 0)
            finish(5, 1)
            band_change(7, 1)
            finish(6, 0)
            finish(7, 1)


_INS = ['x', 'L0_tok_W', 'L0_tok_b', 'L0_tok_gamma', 'L0_tok_beta', 'L0_ffn_fc1_w', 'L0_ffn_fc1_b',
        'L0_ffn_fc2_w', 'L0_ffn_fc2_b']


def _shape_constants():
    import numpy as np
    pos = np.linspace(0.0, 1.0, C, dtype=np.float32) * np.float32(CH - 1)
    i0 = np.clip(np.floor(pos).astype(np.int32), 0, CH - 2)
    w = pos - i0.astype(np.float32)
    a = np.zeros((C, CH), np.float32)
    a[np.arange(C), i0] += np.float32(1.0) - w
    a[np.arange(C), i0 + 1] += w
    half = np.zeros((CH, C), np.float32)
    half[np.arange(C) // 2, np.arange(C)] = 0.5
    return np.concatenate([a, a, np.concatenate([half, half], 0), np.eye(P, dtype=np.float32)], 1)


def kernel(**inputs):
    import numpy as _np
    import concourse.bacc as _bacc
    from concourse import mybir as _mybir
    from concourse.bass_utils import run_bass_kernel_spmd as _run

    nc = _bacc.Bacc("TRN2", target_bir_lowering=False, num_devices=1)
    arrays, args = {}, []
    for name in _INS:
        arrays[f"in_{name}"] = _np.ascontiguousarray(inputs[name])
    arrays["in_consts"] = _shape_constants()
    for name, a in arrays.items():
        args.append(nc.dram_tensor(name, a.shape, _mybir.dt.from_np(a.dtype), kind="ExternalInput").ap())
    args.append(nc.dram_tensor("out", (B, T, C), _mybir.dt.float32, kind="ExternalOutput").ap())
    tower_kernel(nc, *args)
    r = _run(nc, [arrays], core_ids=[0])
    return r.results[0]["out"]
```
